# Optimizing a Trainium2 kernel written in Bass

```python
import numpy as np
import jax
import jax.numpy as jnp

def _softmax(x, axis=-1):
    return jax.nn.softmax(x, axis=axis)

def _gelu(x):
    return jax.nn.gelu(x, approximate=True)

def _silu(x):
    return jax.nn.silu(x)

def _sigmoid(x):
    return jax.nn.sigmoid(x)

def _layernorm(x, axis=-1, eps=1e-05):
    m = jnp.mean(x, axis=axis, keepdims=True)
    v = jnp.var(x, axis=axis, keepdims=True)
    return (x - m) / jnp.sqrt(v + eps)

def _scatter_add(tgt, idx, src, axis=0):
    return tgt.at[idx].add(src)

def _segment_sum(src, seg, n):
    return jax.ops.segment_sum(src, seg, n)
kernel_name = 'mk_adaln_d1_jaxref_r8_9487c3'

def setup_inputs(seed: int=0):
    np.random.seed(seed)
    _w = jnp.asarray

    def _L0_attn_setup():
        import jax, jax.numpy as jnp
        import numpy as np
        H = 128
        I = 512
        TAU = 9
        LN_EPS = 1e-12

        def _l2_normalize(x):
            n = jnp.sqrt(jnp.sum(x * x, axis=-1, keepdims=True))
            return x / jnp.maximum(n, 1e-12)
        key = jax.random.key(seed)
        k1, k2, k3, k4 = jax.random.split(key, 4)
        return {'hidden_states': jax.random.normal(k1, (4, 256, H), jnp.float32), 'ln_weight': jnp.ones((H,), jnp.float32), 'ln_bias': jnp.zeros((H,), jnp.float32), 'k_weight': 0.02 * jax.random.normal(k2, (I, H), jnp.float32), 'q_weight': 0.02 * jax.random.normal(k3, (I, H), jnp.float32), 'bias': 0.001 * jax.random.normal(k4, (H,), jnp.float32)}
    _L0_attn_in = _L0_attn_setup()

    def _L0_ffn_setup():
        import jax, jax.numpy as jnp
        import numpy as np
        B, S, D = (4, 256, 128)
        E = 8
        CF = 1
        key = jax.random.key(seed)
        k_x, k_g, k_w, k_b = jax.random.split(key, 4)
        x = jax.random.normal(k_x, (B, S, D), dtype=jnp.float32)
        Wg = jax.random.normal(k_g, (D, E), dtype=jnp.float32) * (1.0 / np.sqrt(D))
        We = jax.random.normal(k_w, (D, D), dtype=jnp.float32) * (1.0 / np.sqrt(D))
        be = jax.random.normal(k_b, (D,), dtype=jnp.float32) * 0.01
        return {'x': x, 'Wg': Wg, 'We': We, 'be': be}
    _L0_ffn_in = _L0_ffn_setup()
    _L0_c = _w((lambda *s: np.random.randn(*s).astype(np.float32) * 0.05)(4, 128))
    _L0_wmod = _w((lambda *s: np.random.randn(*s).astype(np.float32) * 0.05)(128, 6 * 128) * 128 ** (-0.5))
    _d = {'L0_attn_hidden_states': _L0_attn_in['hidden_states'], 'L0_attn_ln_weight': _L0_attn_in['ln_weight'], 'L0_attn_ln_bias': _L0_attn_in['ln_bias'], 'L0_attn_k_weight': _L0_attn_in['k_weight'], 'L0_attn_q_weight': _L0_attn_in['q_weight'], 'L0_attn_bias': _L0_attn_in['bias'], 'L0_ffn_Wg': _L0_ffn_in['Wg'], 'L0_ffn_We': _L0_ffn_in['We'], 'L0_ffn_be': _L0_ffn_in['be'], 'L0_c': _L0_c, 'L0_wmod': _L0_wmod}
    _x0 = _d['L0_attn_hidden_states']
    _d['L0_attn_hidden_states'] = jax.random.normal(jax.random.fold_in(jax.random.key(seed), 1), (4, 1024, 128), dtype=_x0.dtype)
    del _x0
    return _d

def reference(L0_attn_hidden_states, L0_attn_ln_weight, L0_attn_ln_bias, L0_attn_k_weight, L0_attn_q_weight, L0_attn_bias, L0_ffn_Wg, L0_ffn_We, L0_ffn_be, L0_c, L0_wmod):

    def _L0_attn_ref(hidden_states, ln_weight, ln_bias, k_weight, q_weight, bias):
        import jax, jax.numpy as jnp
        import numpy as np
        H = 128
        I = 512
        TAU = 9
        LN_EPS = 1e-12

        def _l2_normalize(x):
            n = jnp.sqrt(jnp.sum(x * x, axis=-1, keepdims=True))
            return x / jnp.maximum(n, 1e-12)
        lead_shape = hidden_states.shape[:-1]
        x = hidden_states.reshape(-1, H)
        mu = jnp.mean(x, axis=-1, keepdims=True)
        var = jnp.mean(jnp.square(x - mu), axis=-1, keepdims=True)
        x = (x - mu) * jax.lax.rsqrt(var + LN_EPS) * ln_weight + ln_bias
        Q = _l2_normalize(x)
        K = _l2_normalize(k_weight)
        s = jnp.clip(jnp.einsum('nh,ih->ni', Q, K), -1.0 + 1e-06, 1.0 - 1e-06)
        B = jnp.power(1.0 - jnp.arccos(s) / jnp.pi, TAU)
        X = jnp.einsum('ni,ih->nh', B, q_weight)
        X = _l2_normalize(X) + bias
        return X.reshape(*lead_shape, H)

    def _L0_ffn_ref(x, Wg, We, be):
        import jax, jax.numpy as jnp
        import numpy as np
        B, S, D = (4, 256, 128)
        E = 8
        CF = 1
        b, s, d = x.shape
        n = b * s
        cap = n // E * CF
        h = x.reshape(n, d)
        router_logits = h @ Wg
        probs = jax.nn.softmax(router_logits, axis=1)
        best = jnp.argmax(probs, axis=1)
        mask = jax.nn.one_hot(best, E, dtype=probs.dtype)
        gate = jnp.sum(probs * mask, axis=1)
        locations = jnp.cumsum(mask, axis=0) - 1.0
        mask = mask * (locations < cap).astype(mask.dtype)
        loc_idx = jnp.sum(locations * mask, axis=1).astype(jnp.int32)
        new_gate = gate[:, None] * mask
        loc_oh = jax.nn.one_hot(loc_idx, cap, dtype=new_gate.dtype)
        combine = new_gate[:, :, None] * loc_oh[:, None, :]
        dispatch = (combine != 0).astype(h.dtype)
        dispatched = jnp.einsum('nec,nd->ecd', dispatch, h).reshape(E * cap, d)
        expert_out = dispatched @ We + be
        out = combine.reshape(n, E * cap) @ expert_out
        return out.reshape(b, s, d)
    x = L0_attn_hidden_states
    mod = (_silu(L0_c) @ L0_wmod).reshape(L0_c.shape[0], 6, 1, -1)
    sa, ca, ga, sb, cb, gb = (mod[:, 0], mod[:, 1], mod[:, 2], mod[:, 3], mod[:, 4], mod[:, 5])
    ga = (2 * (ga >= 0) - 1) * jnp.maximum(jnp.abs(ga), 0.25)
    gb = (2 * (gb >= 0) - 1) * jnp.maximum(jnp.abs(gb), 0.25)
    h = _layernorm(x, axis=-1) * (1 + ca) + sa
    x = x + ga * _L0_attn_ref(h, L0_attn_ln_weight, L0_attn_ln_bias, L0_attn_k_weight, L0_attn_q_weight, L0_attn_bias)
    h = _layernorm(x, axis=-1) * (1 + cb) + sb
    x = x + gb * _L0_ffn_ref(h, L0_ffn_Wg, L0_ffn_We, L0_ffn_be)
    return x

_drawn_inputs = setup_inputs


def setup_inputs(seed=0):
    import zlib

    import numpy as np

    out = dict(_drawn_inputs(seed))
    spreads = {'L0_attn_ln_weight': (1.0, 0.6), 'L0_attn_ln_bias': (0.0, 2.0)}
    factors = {'L0_attn_k_weight': 93.662, 'L0_attn_bias': 196.727, 'L0_ffn_be': 57.375}
    for name, (base, spread) in spreads.items():
        noise = np.random.default_rng([zlib.crc32(name.encode()), seed]).standard_normal(out[name].shape)
        drawn = base * np.exp(spread * noise) if base else spread * noise
        out[name] = jnp.asarray(drawn.astype(out[name].dtype))
    for name, factor in factors.items():
        out[name] = (out[name] * factor).astype(out[name].dtype)
    return out
```

```python
from contextlib import ExitStack

import concourse.bass as bass
from concourse import mybir

F32 = mybir.dt.float32
BF16 = mybir.dt.bfloat16
ALU = mybir.AluOpType
ACT = mybir.ActivationFunctionType
AX = mybir.AxisListType

P = 128
H = 128
PI = 3.141592653589793
CLIP = 1.0 - 1e-6
TAN_MAX = (1.0 - CLIP * CLIP) ** -0.5
TAU = 9.0
LN_EXP = "natural_log_exp_and_others"
TRIG = "trig_and_small"


def adaln_block(nc, x, ln_weight, ln_bias, k_weight, q_weight, bias, wg, we, be, c, wmod, out):
    NB, T, _ = x.shape
    J = T // P
    HJ = J // 2
    HT = T // 2
    KEYS = k_weight.shape[0]
    KC = KEYS // P
    E = wg.shape[1]
    CAP = float(NB * T // E)
    W = H + E
    PAIRS = 4

    x_rows = x.rearrange("b (p j) h -> b p j h", p=P)
    out_rows = out.rearrange("b (p j) h -> b p j h", p=P)

    with ExitStack() as ctx:
        def sb(name, shape, dt=F32):
            return ctx.enter_context(nc.sbuf_tensor(name, shape, dt))

        def sem(name):
            return ctx.enter_context(nc.semaphore(name))

        score = ctx.enter_context(nc.psum_tensor("score", [P, 4, 512], F32))
        turn = ctx.enter_context(nc.psum_tensor("turn", [P, 512], F32))
        xps = ctx.enter_context(nc.psum_tensor("xps", [P, 512], F32))
        zps = ctx.enter_context(nc.psum_tensor("zps", [P, 2, 512], F32))
        zview = zps[:, :, 0:2 * W].rearrange("p a (t w) -> p a t w", t=2)
        place = zps[:, 0, 384:384 + J * E].rearrange("p (j e) -> p j e", e=E)

        ident = sb("ident", [P, P])
        tri_incl = sb("tri_incl", [P, P], BF16)
        tri_strict = sb("tri_strict", [P, P], BF16)
        ones = sb("ones", [P, P], BF16)
        minus_half = sb("minus_half", [P, J])
        rank = sb("rank", [P, E])
        c_sb = sb("c_sb", [NB, H])
        c_tmp = sb("c_tmp", [NB, 3, H])
        silu_t = sb("silu_t", [P, NB])
        silu_b = sb("silu_b", [P, NB, P])
        wmod_sb = sb("wmod_sb", [P, 6 * H])
        scale1 = sb("scale1", [P, NB, H])
        shift1 = sb("shift1", [P, NB, H])
        gates = sb("gates", [P, NB, 2, H])
        gate_t = sb("gate_t", [P, 3, NB, 2 * H])
        gate_bias = sb("gate_bias", [P, NB, H])
        modc = sb("modc", [P, 2, NB])
        shift2_b = sb("shift2_b", [P, NB, P])
        lnw = sb("lnw", [P, H])
        lnb = sb("lnb", [P, H])
        bias_b = sb("bias_b", [P, H])
        be_b = sb("be_b", [P, H])
        wer = sb("wer", [P, W])
        wer_b = sb("wer_b", [P, NB, W])
        const_b = sb("const_b", [P, NB, W])
        k_sb = sb("k_sb", [P, KC, H])
        k_sq = sb("k_sq", [P, KC, H])
        k_ss = sb("k_ss", [P, 2, KC])
        k_t = sb("k_t", [P, KEYS])
        q_w = sb("q_w", [P, KC, H])

        xin = sb("xin", [P, NB, J, H])
        ya = sb("ya", [P, J, H])
        yh = sb("yh", [P, J, H])
        yg = sb("yg", [P, J, H])
        yq = sb("yq", [P, J, H])
        sq = sb("sq", [P, J, H])
        bn_a = sb("bn_a", [P, J, 6])
        st_a = sb("st_a", [P, J, 2])
        rs_a = sb("rs_a", [P, 2, J])
        bn_a2 = sb("bn_a2", [P, J, 6])
        st_a2 = sb("st_a2", [P, J, 2])
        rs_a2 = sb("rs_a2", [P, 2, J])
        rs_q = sb("rs_q", [P, 2, J])
        q_t = sb("q_t", [P, 2, T])
        root = sb("root", [P, 2, 1024])
        prob = sb("prob", [P, 2, 2, KC, HT])
        xsq = sb("xsq", [P, J, H])
        rs_x = sb("rs_x", [P, 3, J])
        xa = sb("xa", [P, J, H])
        xres = sb("xres", [P, J, H])
        x1 = sb("x1", [P, J, H])
        bn_c = sb("bn_c", [P, J, 6])
        st_c = sb("st_c", [P, J, 2])
        rs_c = sb("rs_c", [P, 2, J])
        yc = sb("yc", [P, J, H])
        y_t = sb("y_t", [P, T])
        z_sb = sb("z_sb", [P, J, H])
        logit = sb("logit", [P, J, E])
        rt = sb("rt", [P, 6, J, E])
        rc = sb("rc", [P, 8, J])
        hot = sb("hot", [P, J, E], BF16)
        taken = sb("taken", [P, 2, E], BF16)
        res = sb("res", [P, J, H])

        x_in = [sem(f"x_in{b}") for b in range(NB)]
        c_in, wmod_in, k_in, qw_in, ln_in, w_in, rows_in = (
            sem(n) for n in ("c_in", "wmod_in", "k_in", "qw_in", "ln_in", "w_in", "rows_in"))
        out_done = sem("out_done")
        pool_const = sem("pool_const")
        silu_exp, silu_row, silu_turn, silu_col, silu_wide = (
            sem(n) for n in ("silu_exp", "silu_row", "silu_turn", "silu_col", "silu_wide"))
        mod_rows, mod_cols, mod1_ready, gate_ready, modc_ready = (
            sem(n) for n in ("mod_rows", "mod_cols", "mod1_ready", "gate_ready", "modc_ready"))
        wer_ready, const_ps, const_ready, gate_bias_ready = (
            sem(n) for n in ("wer_ready", "const_ps", "const_ready", "gate_bias_ready"))
        k_squared, k_summed, k_inv, k_scaled, k_turned, k_ready = (
            sem(n) for n in ("k_squared", "k_summed", "k_inv", "k_scaled", "k_turned", "k_ready"))
        dve_step = sem("dve_step")
        pool_step = sem("pool_step")
        var1_ready, inv1_ready, norm1_ready, h_ready = (
            sem(n) for n in ("var1_ready", "inv1_ready", "norm1_ready", "h_ready"))
        var2_ready, inv2_ready, norm2_ready, g_ready, gsq_ready = (
            sem(n) for n in ("var2_ready", "inv2_ready", "norm2_ready", "g_ready", "gsq_ready"))
        ssq_ready, invq_ready, q_ready, q_turned, q_evac = (
            sem(n) for n in ("ssq_ready", "invq_ready", "q_ready", "q_turned", "q_evac"))
        score_ready, sq_done, ln_done, root_ready, tan_ready = (
            sem(n) for n in ("score_ready", "sq_done", "ln_done", "root_ready", "tan_ready"))
        atan_done, lnp_done, prob_ready = (sem(n) for n in ("atan_done", "lnp_done", "prob_ready"))
        x_ready, xsq_ready, ssx_ready, invx_ready, xres_ready, x1_ready = (
            sem(n) for n in ("x_ready", "xsq_ready", "ssx_ready", "invx_ready", "xres_ready", "x1_ready"))
        xps_used, var3_ready, inv3_ready, y_ready, y_turned, y_evac, z_ready = (
            sem(n) for n in ("xps_used", "var3_ready", "inv3_ready", "y_ready", "y_turned", "y_evac", "z_ready"))
        z_used, below_ready, exp_ready, hot_ready, place_ready, place_used, res_ready = (
            sem(n) for n in ("z_used", "below_ready", "exp_ready", "hot_ready", "place_ready", "place_used", "res_ready"))

        block = ctx.enter_context(nc.Block())

        def row(t, b):
            return t[:, b:b + 1, :].to_broadcast([P, J, H])

        @block.sync
        def _(sp):
            sp.dma_start(c_sb[:, :], c).then_inc(c_in, 16)
            sp.dma_start(wmod_sb[:, :], wmod).then_inc(wmod_in, 16)
            sp.dma_start(xin[:, 0], x_rows[0]).then_inc(x_in[0], 16)
            sp.dma_start(k_sb[:, :, :], k_weight.rearrange("(k p) h -> p k h", p=P)).then_inc(k_in, 16)
            sp.dma_start(xin[:, 1], x_rows[1]).then_inc(x_in[1], 16)
            sp.dma_start(wer[:, 0:H], we).then_inc(w_in, 16)
            sp.dma_start(wer[:, H:W], wg).then_inc(w_in, 16)
            sp.dma_start(q_w[:, :, :], q_weight.rearrange("(k p) h -> p k h", p=P)).then_inc(qw_in, 16)
            for b in range(2, NB):
                sp.dma_start(xin[:, b], x_rows[b]).then_inc(x_in[b], 16)
            for b in range(NB):
                sp.wait_ge(res_ready, b + 1)
                sp.dma_start(out_rows[b], res[:, :, :]).then_inc(out_done, 16)
            sp.wait_ge(out_done, 16 * NB)

        @block.gpsimd
        def _(pool):
            step = [0]

            def link(ins):
                step[0] += 1
                ins.then_inc(pool_step, 1)
                pool.wait_ge(pool_step, step[0])

            pool.memset(ident[:, :], 0.0).then_inc(pool_const, 1)
            pool.memset(ones[:, :], 1.0).then_inc(pool_const, 1)
            pool.memset(minus_half[:, :], -0.5).then_inc(pool_const, 1)
            pool.wait_ge(pool_const, 3)
            pool.affine_select(out=ident[:, :], in_=ident[:, :], compare_op=ALU.not_equal, fill=1.0,
                               base=0, pattern=[[-1, P]], channel_multiplier=1).then_inc(pool_const, 1)
            pool.affine_select(out=tri_incl[:, :], in_=ones[:, :], compare_op=ALU.is_ge, fill=0.0,
                               base=0, pattern=[[1, P]], channel_multiplier=-1).then_inc(pool_const, 1)
            pool.affine_select(out=tri_strict[:, :], in_=ones[:, :], compare_op=ALU.is_gt, fill=0.0,
                               base=0, pattern=[[1, P]], channel_multiplier=-1).then_inc(pool_const, 1)
            for e in range(E):
                pool.memset(rank[:, e:e + 1], float(E - e)).then_inc(pool_const, 1)

            def inv_root(dst, src, ready, count, signal):
                pool.wait_ge(ready, count)
                pool.tensor_tensor(dst, src, minus_half[:, 0:src.shape[1]], ALU.pow).then_inc(signal, 1)

            def keys():
                pool.wait_ge(k_in, 16)
                pool.tensor_tensor(k_sq[:, :, :], k_sb[:, :, :], k_sb[:, :, :], ALU.mult).then_inc(k_squared, 1)
                inv_root(k_ss[:, 1, :], k_ss[:, 0, :], k_summed, 1, k_inv)

            def stage_a1(b):
                inv_root(rs_a[:, 1, :], rs_a[:, 0, :], var1_ready, b + 1, inv1_ready)

            def stage_a2(b):
                if b == 0:
                    pool.wait_ge(mod1_ready, 1)
                pool.wait_ge(norm1_ready, b + 1)
                if b > 0:
                    pool.wait_ge(norm2_ready, b)
                link(pool.tensor_tensor(yh[:, :, :], ya[:, :, :], row(scale1, b), ALU.mult))
                pool.tensor_tensor(yh[:, :, :], yh[:, :, :], row(shift1, b), ALU.add).then_inc(h_ready, 1)

            def stage_a3(b):
                inv_root(rs_a2[:, 1, :], rs_a2[:, 0, :], var2_ready, b + 1, inv2_ready)

            def stage_a4(b):
                if b == 0:
                    pool.wait_ge(ln_in, 32)
                pool.wait_ge(norm2_ready, b + 1)
                wide = [lnw[:, :].unsqueeze(1).to_broadcast([P, J, H]), lnb[:, :].unsqueeze(1).to_broadcast([P, J, H])]
                link(pool.tensor_tensor(yg[:, :, :], yg[:, :, :], wide[0], ALU.mult))
                link(pool.tensor_tensor(yg[:, :, :], yg[:, :, :], wide[1], ALU.add))
                if b > 0:
                    pool.wait_ge(ssq_ready, b)
                pool.tensor_tensor(sq[:, :, :], yg[:, :, :], yg[:, :, :], ALU.mult).then_inc(gsq_ready, 1)
                inv_root(rs_q[:, 1, :], rs_q[:, 0, :], ssq_ready, b + 1, invq_ready)

            def stage_x(b):
                if b == 0:
                    pool.wait_ge(gate_bias_ready, 1)
                else:
                    pool.wait_ge(x1_ready, b)
                pool.wait_ge(x_in[b], 16)
                pool.tensor_tensor(xres[:, :, :], xin[:, b], row(gate_bias, b), ALU.add).then_inc(xres_ready, 1)

            keys()
            for b in range(NB + 1):
                if b == 0:
                    stage_a1(0)
                    stage_a2(0)
                    stage_a3(0)
                    stage_a4(0)
                if b + 1 < NB:
                    stage_a1(b + 1)
                    stage_a2(b + 1)
                if b > 0:
                    stage_x(b - 1)
                    inv_root(rs_x[:, 1, :], rs_x[:, 0, :], ssx_ready, b, invx_ready)
                if b + 1 < NB:
                    stage_a3(b + 1)
                if b > 0:
                    inv_root(rs_c[:, 1, :], rs_c[:, 0, :], var3_ready, b, inv3_ready)
                if b + 1 < NB:
                    stage_a4(b + 1)

        @block.scalar
        def _(act):
            act.dma_start(lnw[:, :], ln_weight.partition_broadcast(P)).then_inc(ln_in, 16)
            act.dma_start(lnb[:, :], ln_bias.partition_broadcast(P)).then_inc(ln_in, 16)
            act.dma_start(bias_b[:, :], bias.partition_broadcast(P)).then_inc(rows_in, 16)
            act.dma_start(be_b[:, :], be.partition_broadcast(P)).then_inc(rows_in, 16)
            act.preload_act_table_set(LN_EXP)
            act.wait_ge(c_in, 16)
            act.activation(c_tmp[:, 0, :], c_sb[:, :], ACT.Exp, scale=-1.0).then_inc(silu_exp, 1)

            def roots(b, p):
                n = PAIRS * b + p
                r = root[:, n % 2, :]
                act.wait_ge(score_ready, n + 1)
                if n >= 2:
                    act.wait_ge(tan_ready, n - 1)
                act.activation(r.rearrange("p (a t) -> p a t", a=2), score[:, 2 * (n % 2):2 * (n % 2) + 2, :],
                               ACT.Square).then_inc(sq_done, 1)
                act.wait_ge(sq_done, n + 1)
                act.activation(r, r, ACT.Ln, scale=-1.0, bias=1.0).then_inc(ln_done, 1)
                act.wait_ge(ln_done, n + 1)
                act.activation(r, r, ACT.Exp, scale=-0.5).then_inc(root_ready, 1)

            def x_square(b, h):
                n = 2 * b + h
                act.wait_ge(x_ready, n + 1)
                if h == 0 and b > 0:
                    act.wait_ge(ssx_ready, b)
                act.activation(xsq[:, h * HJ:(h + 1) * HJ, :], xps[:, :].rearrange("p (j h) -> p j h", h=H),
                               ACT.Square).then_inc(xsq_ready, 1)

            def y_copy(b, h):
                n = 2 * b + h
                act.wait_ge(y_turned, n + 1)
                if b > 0:
                    act.wait_ge(z_ready, n - 1)
                act.activation(y_t[:, h * HT:(h + 1) * HT], turn[:, :], ACT.Copy).then_inc(y_evac, 1)

            def angle(b, h):
                t = prob[:, b % 2, h].rearrange("p k t -> p (k t)")
                act.wait_ge(tan_ready, PAIRS * b + 2 * h + 2)
                act.activation(t, t, ACT.Arctan).then_inc(atan_done, 1)

            def power(b, h):
                n = 2 * b + h
                t = prob[:, b % 2, h].rearrange("p k t -> p (k t)")
                act.wait_ge(atan_done, n + 1)
                act.activation(t, t, ACT.Ln, scale=1.0 / PI, bias=0.5).then_inc(lnp_done, 1)
                act.wait_ge(lnp_done, n + 1)
                act.activation(t, t, ACT.Exp, scale=TAU).then_inc(prob_ready, 1)

            for b in range(NB + 1):
                if b < NB:
                    roots(b, 0)
                if b > 0:
                    x_square(b - 1, 0)
                if b < NB:
                    roots(b, 1)
                if b > 0:
                    x_square(b - 1, 1)
                if b < NB:
                    roots(b, 2)
                    roots(b, 3)
                if b > 0:
                    y_copy(b - 1, 0)
                    y_copy(b - 1, 1)
                if b < NB:
                    act.preload_act_table_set(TRIG)
                    angle(b, 0)
                    angle(b, 1)
                    act.preload_act_table_set(LN_EXP)
                if b > 0:
                    act.wait_ge(below_ready, b)
                    act.activation(rt[:, 1], rt[:, 0], ACT.Exp).then_inc(exp_ready, 1)
                if b < NB:
                    power(b, 0)
                    power(b, 1)

        @block.vector
        def _(dve):
            step = [0]

            def link(ins):
                step[0] += 1
                ins.then_inc(dve_step, 1)
                dve.wait_ge(dve_step, step[0])

            dve.wait_ge(silu_exp, 1)
            link(dve.tensor_scalar(c_tmp[:, 1, :], c_tmp[:, 0, :], 1.0, None, ALU.add))
            link(dve.reciprocal(c_tmp[:, 2, :], c_tmp[:, 1, :]))
            dve.tensor_tensor(c_sb[:, :], c_sb[:, :], c_tmp[:, 2, :], ALU.mult).then_inc(silu_row, 1)
            dve.wait_ge(silu_turn, 1)
            dve.tensor_copy(silu_t[:, :], turn[:, 0:NB]).then_inc(silu_col, 1)
            dve.wait_ge(silu_col, 1)
            dve.tensor_copy(silu_b[:, :, :], silu_t[:, :].unsqueeze(2).to_broadcast([P, NB, P])).then_inc(silu_wide, 1)

            def stats(rows, bn, st, var, eps, signal):
                for j in range(J):
                    last = dve.bn_stats(bn[:, j, :], rows[:, j, :])
                link(last)
                for j in range(J):
                    last = dve.bn_aggr(st[:, j, :], bn[:, j, :])
                link(last)
                dve.tensor_scalar(var, st[:, :, 1], eps, None, ALU.add).then_inc(signal, 1)

            def normed(dst, rows, st, inv, signal):
                for j in range(J):
                    last = dve.tensor_scalar(dst[:, j, :], rows[:, j, :], st[:, j, 0:1], inv[:, j:j + 1],
                                             ALU.subtract, ALU.mult)
                last.then_inc(signal, 1)

            def stage_a1(b):
                dve.wait_ge(x_in[b], 16)
                stats(xin[:, b], bn_a, st_a, rs_a[:, 0, :], 1e-5, var1_ready)

            def stage_a2(b):
                dve.wait_ge(inv1_ready, b + 1)
                if b > 0:
                    dve.wait_ge(h_ready, b)
                normed(ya, xin[:, b], st_a, rs_a[:, 1, :], norm1_ready)

            def stage_a3(b):
                dve.wait_ge(h_ready, b + 1)
                stats(yh, bn_a2, st_a2, rs_a2[:, 0, :], 1e-12, var2_ready)

            def stage_a4(b):
                dve.wait_ge(inv2_ready, b + 1)
                normed(yg, yh, st_a2, rs_a2[:, 1, :], norm2_ready)

            def stage_a5(b):
                dve.wait_ge(gsq_ready, b + 1)
                link(dve.tensor_reduce(rs_q[:, 0, :], sq[:, :, :], AX.X, ALU.add))
                dve.tensor_scalar(rs_q[:, 0, :], rs_q[:, 0, :], 1e-24, None, ALU.max).then_inc(ssq_ready, 1)

            def stage_a6(b):
                dve.wait_ge(invq_ready, b + 1)
                if b > 0:
                    dve.wait_ge(q_turned, 2 * b)
                for j in range(J):
                    last = dve.tensor_scalar(yq[:, j, :], yg[:, j, :], rs_q[:, 1, j:j + 1], None, ALU.mult)
                last.then_inc(q_ready, 1)
                for h in range(2):
                    dve.wait_ge(q_turned, 2 * b + h + 1)
                    if b > 1:
                        dve.wait_ge(score_ready, PAIRS * (b - 1))
                    dve.tensor_copy(q_t[:, b % 2, h * HT:(h + 1) * HT], turn[:, :]).then_inc(q_evac, 1)

            def tangent(b, p):
                n = PAIRS * b + p
                dve.wait_ge(root_ready, n + 1)
                if b > 1 and p % 2 == 0:
                    dve.wait_ge(x_ready, 2 * (b - 2) + p // 2 + 1)
                dve.scalar_tensor_tensor(out=prob[:, b % 2, p // 2, 2 * (p % 2):2 * (p % 2) + 2, :],
                                         in0=root[:, n % 2, :].rearrange("p (a t) -> p a t", a=2), scalar=TAN_MAX,
                                         in1=score[:, 2 * (n % 2):2 * (n % 2) + 2, :],
                                         op0=ALU.min, op1=ALU.mult).then_inc(tan_ready, 1)

            def keys_sum():
                dve.wait_ge(k_squared, 1)
                link(dve.tensor_reduce(k_ss[:, 0, :], k_sq[:, :, :], AX.X, ALU.add))
                dve.tensor_scalar(k_ss[:, 0, :], k_ss[:, 0, :], 1e-24, None, ALU.max).then_inc(k_summed, 1)

            def keys_scale():
                dve.wait_ge(k_inv, 1)
                for k in range(KC):
                    last = dve.tensor_scalar(k_sb[:, k, :], k_sb[:, k, :], k_ss[:, 1, k:k + 1], None, ALU.mult)
                last.then_inc(k_scaled, 1)

            def keys_copy():
                dve.wait_ge(k_turned, 1)
                dve.tensor_copy(k_t[:, :], xps[:, :]).then_inc(k_ready, 1)

            def first_rows():
                dve.wait_ge(mod_rows, 1)
                dve.tensor_scalar(scale1[:, :, :], score[:, :, H:2 * H], 1.0, None, ALU.add)
                dve.tensor_copy(shift1[:, :, :], score[:, :, 0:H]).then_inc(mod1_ready, 1)

            def gate_rows():
                g = score[:, :, 2 * H:4 * H]
                two, sign, size = (gate_t[:, i] for i in range(3))
                link(dve.tensor_scalar(two, g, 0.0, 2.0, ALU.is_ge, ALU.mult))
                link(dve.tensor_scalar(sign, two, -1.0, None, ALU.add))
                link(dve.tensor_tensor(size, g, sign, ALU.mult))
                dve.scalar_tensor_tensor(out=gates[:, :, :, :].rearrange("p b g h -> p b (g h)"), in0=size,
                                         scalar=0.25, in1=sign, op0=ALU.max, op1=ALU.mult).then_inc(gate_ready, 1)

            def mod_columns():
                dve.wait_ge(mod_cols, 1)
                dve.tensor_copy(modc[:, 0, :], turn[:, 0:NB])
                dve.tensor_scalar(modc[:, 1, :], turn[:, NB:2 * NB], 1.0, None, ALU.add).then_inc(modc_ready, 1)
                dve.wait_ge(modc_ready, 1)
                dve.tensor_copy(shift2_b[:, :, :], modc[:, 0, :].unsqueeze(2).to_broadcast([P, NB, P])).then_inc(modc_ready, 1)

            def fold_weights():
                dve.wait_ge(rows_in, 32)
                dve.wait_ge(gate_ready, 1)
                dve.tensor_tensor(gate_bias[:, :, :], gates[:, :, 0, :],
                                  bias_b[:, :].unsqueeze(1).to_broadcast([P, NB, H]), ALU.mult).then_inc(gate_bias_ready, 1)
                dve.wait_ge(w_in, 32)
                for b in range(NB):
                    dve.scalar_tensor_tensor(out=wer_b[:, b, 0:H], in0=wer[:, 0:H], scalar=modc[:, 1, b:b + 1],
                                             in1=gates[:, b, 1, :], op0=ALU.mult, op1=ALU.mult)
                    last = dve.tensor_scalar(wer_b[:, b, H:W], wer[:, H:W], modc[:, 1, b:b + 1], None, ALU.mult)
                last.then_inc(wer_ready, 1)
                dve.wait_ge(const_ps, 1)
                for b in range(NB):
                    z = zview[:, b // 2, b % 2, :]
                    dve.tensor_tensor(const_b[:, b, 0:H], z[:, 0:H], be_b[:, :], ALU.add)
                    last = dve.tensor_copy(const_b[:, b, H:W], z[:, H:W])
                link(last)
                dve.tensor_tensor(const_b[:, :, 0:H], const_b[:, :, 0:H], gates[:, :, 1, :], ALU.mult).then_inc(const_ready, 1)

            def stage_c1(b):
                dve.wait_ge(xsq_ready, 2 * b + 2)
                link(dve.tensor_reduce(rs_x[:, 0, :], xsq[:, :, :], AX.X, ALU.add))
                dve.tensor_scalar(rs_x[:, 0, :], rs_x[:, 0, :], 1e-24, None, ALU.max).then_inc(ssx_ready, 1)

            def evac_x(b, h):
                n = 2 * b + h
                dve.wait_ge(x_ready, n + 1)
                dve.wait_ge(xsq_ready, n + 1)
                dve.tensor_tensor(xa[:, h * HJ:(h + 1) * HJ, :], xps[:, :].rearrange("p (j h) -> p j h", h=H),
                                  gates[:, b, 0:1, :].to_broadcast([P, HJ, H]), ALU.mult).then_inc(xps_used, 1)

            def stage_c2(b):
                dve.wait_ge(invx_ready, b + 1)
                dve.wait_ge(xres_ready, b + 1)
                for j in range(J):
                    last = dve.scalar_tensor_tensor(out=x1[:, j, :], in0=xa[:, j, :], scalar=rs_x[:, 1, j:j + 1],
                                                    in1=xres[:, j, :], op0=ALU.mult, op1=ALU.add)
                last.then_inc(x1_ready, 1)

            def stage_c3(b):
                dve.wait_ge(x1_ready, b + 1)
                stats(x1, bn_c, st_c, rs_c[:, 0, :], 1e-5, var3_ready)

            def stage_c4(b):
                dve.wait_ge(inv3_ready, b + 1)
                if b > 0:
                    dve.wait_ge(y_turned, 2 * b)
                normed(yc, x1, st_c, rs_c[:, 1, :], y_ready)

            def evac_z(b, h):
                dve.wait_ge(z_ready, 2 * b + h + 1)
                s = slice(h * HJ, (h + 1) * HJ)
                for i in range(2):
                    t = slice(h * HJ + 2 * i, h * HJ + 2 * i + 2)
                    dve.tensor_tensor(logit[:, t, :], zview[:, i, :, H:W],
                                      const_b[:, b:b + 1, H:W].to_broadcast([P, 2, E]), ALU.add)
                    last = dve.tensor_tensor(z_sb[:, t, :], zview[:, i, :, 0:H],
                                             const_b[:, b:b + 1, 0:H].to_broadcast([P, 2, H]), ALU.add)
                last.then_inc(z_used, 1)

            def wide(col):
                return col.unsqueeze(2).to_broadcast([P, J, E])

            def router1(b):
                dve.wait_ge(z_used, 2 * b + 2)
                link(dve.tensor_reduce(rc[:, 0, :], logit[:, :, :], AX.X, ALU.max))
                dve.tensor_tensor(rt[:, 0], logit[:, :, :], wide(rc[:, 0, :]), ALU.subtract).then_inc(below_ready, 1)
                link(dve.tensor_tensor(rt[:, 2], logit[:, :, :], wide(rc[:, 0, :]), ALU.is_equal))
                link(dve.tensor_tensor(rt[:, 3], rt[:, 2], rank[:, :].unsqueeze(1).to_broadcast([P, J, E]), ALU.mult))
                link(dve.tensor_reduce(rc[:, 1, :], rt[:, 3], AX.X, ALU.max))
                if b > 0:
                    dve.wait_ge(place_ready, b)
                link(dve.tensor_tensor(hot[:, :, :], rt[:, 3], wide(rc[:, 1, :]), ALU.is_equal))
                link(dve.tensor_reduce(rt[:, 4, 0, :], hot[:, :, :].rearrange("p j e -> p e j"), AX.X, ALU.add))
                dve.tensor_tensor(taken[:, (b + 1) % 2, :], taken[:, b % 2, :], rt[:, 4, 0, :], ALU.add).then_inc(hot_ready, 1)

            def router2(b):
                dve.wait_ge(exp_ready, b + 1)
                link(dve.tensor_reduce(rc[:, 2, :], rt[:, 1], AX.X, ALU.add))
                link(dve.reciprocal(rc[:, 3, :], rc[:, 2, :]))
                dve.wait_ge(place_ready, b + 1)
                link(dve.scalar_tensor_tensor(out=rt[:, 5], in0=place, scalar=CAP, in1=hot[:, :, :],
                                              op0=ALU.is_le, op1=ALU.mult))
                link(dve.tensor_reduce(rc[:, 4, :], rt[:, 5], AX.X, ALU.add))
                link(dve.tensor_tensor(rc[:, 5, :], rc[:, 4, :], rc[:, 3, :], ALU.mult))
                if b > 0:
                    dve.wait_ge(out_done, 16 * b)
                for j in range(J):
                    last = dve.scalar_tensor_tensor(out=res[:, j, :], in0=z_sb[:, j, :], scalar=rc[:, 5, j:j + 1],
                                                    in1=x1[:, j, :], op0=ALU.mult, op1=ALU.add)
                last.then_inc(res_ready, 1)

            dve.memset(taken[:, :, :], 0.0)
            stage_a1(0)
            keys_sum()
            stage_a2(0)
            first_rows()
            mod_columns()
            keys_scale()
            keys_copy()
            stage_a3(0)
            gate_rows()
            stage_a4(0)
            stage_a5(0)
            stage_a6(0)
            fold_weights()
            for b in range(NB + 1):
                now, ahead, behind = b < NB, b + 1 < NB, b > 0
                if now:
                    tangent(b, 0)
                if ahead:
                    stage_a1(b + 1)
                if behind:
                    evac_x(b - 1, 0)
                if now:
                    tangent(b, 1)
                if behind:
                    evac_x(b - 1, 1)
                    stage_c1(b - 1)
                if ahead:
                    stage_a2(b + 1)
                if now:
                    tangent(b, 2)
                if behind:
                    stage_c2(b - 1)
                    stage_c3(b - 1)
                if now:
                    tangent(b, 3)
                if ahead:
                    stage_a3(b + 1)
                if behind:
                    stage_c4(b - 1)
                if ahead:
                    stage_a4(b + 1)
                if behind:
                    evac_z(b - 1, 0)
                    evac_z(b - 1, 1)
                    router1(b - 1)
                if ahead:
                    stage_a5(b + 1)
                    stage_a6(b + 1)
                if behind:
                    router2(b - 1)

        @block.tensor
        def _(pe):
            pe.wait_ge(silu_row, 1)
            pe.wait_ge(pool_const, 4)
            pe.transpose(turn[:, 0:NB], c_sb[:, :], ident[0:NB, 0:NB]).then_inc(silu_turn, 1)
            pe.wait_ge(silu_wide, 1)
            pe.wait_ge(wmod_in, 16)
            for b in range(NB):
                pe.matmul(score[:, b, 0:3 * H], silu_b[:, b, :], wmod_sb[:, 0:3 * H], start=True, stop=True)
                last = pe.matmul(score[:, b, 3 * H:4 * H], silu_b[:, b, :], wmod_sb[:, 5 * H:6 * H], start=True, stop=True)
            last.then_inc(mod_rows, 1)
            for i in range(2):
                last = pe.matmul(turn[:, i * NB:(i + 1) * NB], wmod_sb[:, (3 + i) * H:(4 + i) * H], silu_t[:, :],
                                 start=True, stop=True)
            last.then_inc(mod_cols, 1)
            pe.wait_ge(k_scaled, 1)
            for k in range(KC):
                last = pe.transpose(xps[:, k * P:(k + 1) * P], k_sb[:, k, :], ident[:, :])
            last.then_inc(k_turned, 1)

            def turn_rows(rows, h, signal):
                for j in range(HJ):
                    last = pe.transpose(turn[:, j * P:(j + 1) * P], rows[:, h * HJ + j, :], ident[:, :])
                last.then_inc(signal, 1)

            def turn_q(b):
                pe.wait_ge(q_ready, b + 1)
                for h in range(2):
                    if b == 0 and h == 0:
                        pe.wait_ge(modc_ready, 1)
                    if b + h > 0:
                        pe.wait_ge(q_evac, 2 * b + h)
                    if b > 1:
                        pe.wait_ge(y_evac, 2 * (b - 1))
                    turn_rows(yq, h, q_turned)

            def scores(b, p):
                n = PAIRS * b + p
                if p == 0:
                    pe.wait_ge(q_evac, 2 * b + 1)
                if p == 2:
                    pe.wait_ge(q_evac, 2 * b + 2)
                if n == 0:
                    pe.wait_ge(k_ready, 1)
                    pe.wait_ge(gate_ready, 1)
                if n >= 2:
                    pe.wait_ge(tan_ready, n - 1)
                for i in range(2):
                    k = 2 * (p % 2) + i
                    last = pe.matmul(score[:, 2 * (n % 2) + i, :], k_t[:, k * P:(k + 1) * P],
                                     q_t[:, b % 2, (p // 2) * HT:(p // 2 + 1) * HT], start=True, stop=True)
                last.then_inc(score_ready, 1)

            def attend(b, h):
                n = 2 * b + h
                pe.wait_ge(prob_ready, n + 1)
                if n == 0:
                    pe.wait_ge(qw_in, 16)
                else:
                    pe.wait_ge(xps_used, n)
                for j in range(HJ):
                    for k in range(KC):
                        last = pe.matmul(xps[:, j * H:(j + 1) * H], prob[:, b % 2, h, k, j * P:(j + 1) * P],
                                         q_w[:, k, :], start=(k == 0), stop=(k == KC - 1))
                last.then_inc(x_ready, 1)

            def project(b, h):
                n = 2 * b + h
                if h == 0:
                    pe.wait_ge(y_ready, b + 1)
                    if b + 1 < NB:
                        pe.wait_ge(q_evac, 2 * b + 4)
                if n > 0:
                    pe.wait_ge(y_evac, n)
                turn_rows(yc, h, y_turned)
                pe.wait_ge(y_evac, n + 1)
                if n == 0:
                    pe.wait_ge(const_ready, 1)
                    pe.wait_ge(wer_ready, 1)
                else:
                    pe.wait_ge(z_used, n)
                for j in range(HJ):
                    last = pe.matmul(zview[:, j // 2, j % 2, :], y_t[:, (h * HJ + j) * P:(h * HJ + j + 1) * P],
                                     wer_b[:, b, :], start=True, stop=True)
                last.then_inc(z_ready, 1)

            def queue(b):
                pe.wait_ge(hot_ready, b + 1)
                if b == 0:
                    pe.wait_ge(pool_const, 6)
                pe.matmul(place, ones[:, :], taken[:, b % 2, :].unsqueeze(1).to_broadcast([P, J, E]),
                          start=True, stop=False)
                for j in range(J):
                    if j > 0:
                        pe.matmul(place[:, 0:j, :], tri_strict[:, :], hot[:, j:j + 1, :].to_broadcast([P, j, E]),
                                  start=False, stop=False)
                    last = pe.matmul(place[:, j:J, :], tri_incl[:, :], hot[:, j:j + 1, :].to_broadcast([P, J - j, E]),
                                     start=False, stop=(j == J - 1))
                last.then_inc(place_ready, 1)

            def constants():
                pe.wait_ge(modc_ready, 2)
                pe.wait_ge(w_in, 32)
                for b in range(NB):
                    last = pe.matmul(zview[:, b // 2, b % 2, :], shift2_b[:, b, :], wer[:, :], start=True, stop=True)
                last.then_inc(const_ps, 1)

            turn_q(0)
            scores(0, 0)
            scores(0, 1)
            constants()
            scores(0, 2)
            scores(0, 3)
            for b in range(NB):
                if b + 1 < NB:
                    turn_q(b + 1)
                    scores(b + 1, 0)
                    scores(b + 1, 1)
                if b > 0:
                    queue(b - 1)
                attend(b, 0)
                attend(b, 1)
                if b + 1 < NB:
                    scores(b + 1, 2)
                    scores(b + 1, 3)
                project(b, 0)
                project(b, 1)
            queue(NB - 1)


_INS = ["L0_attn_hidden_states", "L0_attn_ln_weight", "L0_attn_ln_bias", "L0_attn_k_weight", "L0_attn_q_weight",
        "L0_attn_bias", "L0_ffn_Wg", "L0_ffn_We", "L0_ffn_be", "L0_c", "L0_wmod"]


def kernel(**inputs):
    import numpy as _np
    import concourse.bacc as _bacc
    from concourse import mybir as _mybir
    from concourse.bass_utils import run_bass_kernel_spmd as _run

    nc = _bacc.Bacc("TRN2", target_bir_lowering=False, num_devices=1)
    arrays, args = {}, []
    for name in _INS:
        a = _np.ascontiguousarray(inputs[name])
        arrays[f"in_{name}_dram"] = a
        args.append(nc.dram_tensor(f"in_{name}_dram", a.shape, _mybir.dt.from_np(a.dtype), kind="ExternalInput").ap())
    shape = inputs["L0_attn_hidden_states"].shape
    out = nc.dram_tensor("out_0_dram", tuple(shape), _mybir.dt.from_np(_np.dtype("float32")), kind="ExternalOutput").ap()
    adaln_block(nc, *args, out)
    r = _run(nc, [arrays], core_ids=[0])
    return r.results[0]["out_0_dram"]
```

```python
from contextlib import ExitStack

import concourse.bass as bass
from concourse import mybir

F32 = mybir.dt.float32
BF16 = mybir.dt.bfloat16
ALU = mybir.AluOpType
ACT = mybir.ActivationFunctionType
AX = mybir.AxisListType

P = 128
H = 128
PI = 3.141592653589793
CLIP = 1.0 - 1e-6
TAN_MAX = (1.0 - CLIP * CLIP) ** -0.5
TAU = 9.0
LN_EXP = "natural_log_exp_and_others"
TRIG = "trig_and_small"


def adaln_block(nc, x, ln_weight, ln_bias, k_weight, q_weight, bias, wg, we, be, c, wmod, out):
    NB, T, _ = x.shape
    J = T // P
    HJ = J // 2
    HT = T // 2
    KEYS = k_weight.shape[0]
    KC = KEYS // P
    E = wg.shape[1]
    CAP = float(NB * T // E)
    W = H + E
    U = 2 * NB

    x_rows = x.rearrange("b (p j) h -> b p j h", p=P)
    out_rows = out.rearrange("b (p j) h -> b p j h", p=P)

    with ExitStack() as ctx:
        def sb(name, shape, dt=F32):
            return ctx.enter_context(nc.sbuf_tensor(name, shape, dt))

        def sem(name):
            return ctx.enter_context(nc.semaphore(name))

        score = ctx.enter_context(nc.psum_tensor("score", [P, 4, 512], F32))
        turn = ctx.enter_context(nc.psum_tensor("turn", [P, 512], F32))
        xps = ctx.enter_context(nc.psum_tensor("xps", [P, 512], F32))
        zps = ctx.enter_context(nc.psum_tensor("zps", [P, 2, 512], F32))
        zview = zps[:, :, 0:2 * W].rearrange("p a (t w) -> p a t w", t=2)
        place = zps[:, 0, 384:384 + J * E].rearrange("p (j e) -> p j e", e=E)

        ident = sb("ident", [P, P])
        tri_incl = sb("tri_incl", [P, P], BF16)
        tri_strict = sb("tri_strict", [P, P], BF16)
        ones = sb("ones", [P, P], BF16)
        minus_half = sb("minus_half", [P, J])
        rank = sb("rank", [P, E])
        c_sb = sb("c_sb", [NB, H])
        c_silu = sb("c_silu", [NB, H])
        c_tmp = sb("c_tmp", [NB, 3, H])
        silu_t = sb("silu_t", [P, NB])
        silu_b = sb("silu_b", [P, NB, P])
        wmod_sb = sb("wmod_sb", [P, 6 * H])
        mod_row = sb("mod_row", [P, NB, 4, H])
        gates = sb("gates", [P, NB, 2, H])
        gate_t = sb("gate_t", [P, 3, NB, 2, H])
        gate_bias = sb("gate_bias", [P, NB, H])
        modc = sb("modc", [P, 2, NB])
        shift2_b = sb("shift2_b", [P, NB, P])
        lnw = sb("lnw", [P, H])
        lnb = sb("lnb", [P, H])
        bias_b = sb("bias_b", [P, H])
        be_b = sb("be_b", [P, H])
        wer = sb("wer", [P, W])
        wer_b = sb("wer_b", [P, NB, W])
        const_b = sb("const_b", [P, NB, W])
        k_sb = sb("k_sb", [P, KC, H])
        k_sq = sb("k_sq", [P, KC, H])
        k_unit = sb("k_unit", [P, KC, H])
        k_ss = sb("k_ss", [P, 3, KC])
        k_t = sb("k_t", [P, KEYS])
        q_w = sb("q_w", [P, KC, H])

        xin = sb("xin", [P, NB, J, H])
        ya = sb("ya", [P, 2, HJ, H])
        yh = sb("yh", [P, 2, HJ, H])
        yg = sb("yg", [P, 2, HJ, H])
        gsq = sb("gsq", [P, 2, HJ, H])
        yq = sb("yq", [P, 2, HJ, H])
        bn = sb("bn", [P, 3, HJ, 6])
        st = sb("st", [P, 3, 2, HJ, 2])
        rs = sb("rs", [P, 5, 2, 2, HJ])
        ss = sb("ss", [P, 2, HJ])
        q_t = sb("q_t", [P, 2, T])
        root = sb("root", [P, 2, 1024])
        prob = sb("prob", [P, 2, 2, KC, HT])
        xsq = sb("xsq", [P, 2, HJ, H])
        xa = sb("xa", [P, 2, HJ, H])
        xres = sb("xres", [P, 2, HJ, H])
        x1 = sb("x1", [P, 2, J, H])
        yc = sb("yc", [P, 2, HJ, H])
        y_t = sb("y_t", [P, 2, HT])
        z_sb = sb("z_sb", [P, 2, J, H])
        logit = sb("logit", [P, 2, J, E])
        rt = sb("rt", [P, 6, J, E])
        rc = sb("rc", [P, 6, J])
        keep_gate = sb("keep_gate", [P, 2, J])
        hot = sb("hot", [P, J, E], BF16)
        taken = sb("taken", [P, 2, E], BF16)
        res = sb("res", [P, 2, J, H])

        x_in = [sem(f"x_in{b}") for b in range(NB)]
        c_in, wmod_in, k_in, qw_in, ln_in, w_in, rows_in = (
            sem(n) for n in ("c_in", "wmod_in", "k_in", "qw_in", "ln_in", "w_in", "rows_in"))
        out_done = [sem(f"out_done{b}") for b in range(NB)]
        pool_const = sem("pool_const")
        dve_step = sem("dve_step")
        pool_step = sem("pool_step")
        silu_exp, silu_row, silu_turn, silu_col, silu_wide = (
            sem(n) for n in ("silu_exp", "silu_row", "silu_turn", "silu_col", "silu_wide"))
        mod_ps, mod_cols, mod_rows, gate_ready, gate_bias_ready, modc_ready, shift2_ready = (
            sem(n) for n in ("mod_ps", "mod_cols", "mod_rows", "gate_ready", "gate_bias_ready", "modc_ready",
                             "shift2_ready"))
        wer_ready, const_ps, const_ready = (sem(n) for n in ("wer_ready", "const_ps", "const_ready"))
        k_squared, k_summed, k_inv, k_scaled, k_turned, k_ready = (
            sem(n) for n in ("k_squared", "k_summed", "k_inv", "k_scaled", "k_turned", "k_ready"))
        var_ready = [sem(f"var{i}_ready") for i in range(3)]
        inv_ready = [sem(f"inv{i}_ready") for i in range(3)]
        norm1_ready, h_ready, norm2_ready, g_ready, ssq_ready, invq_ready = (
            sem(n) for n in ("norm1_ready", "h_ready", "norm2_ready", "g_ready", "ssq_ready", "invq_ready"))
        q_ready, q_turned, q_evac = (sem(n) for n in ("q_ready", "q_turned", "q_evac"))
        score_ready, sq_done, ln_done, root_ready, tan_ready = (
            sem(n) for n in ("score_ready", "sq_done", "ln_done", "root_ready", "tan_ready"))
        atan_done, lnp_done, prob_ready = (sem(n) for n in ("atan_done", "lnp_done", "prob_ready"))
        x_ready, xsq_ready, xps_used, ssx_ready, invx_ready, xres_ready, x1_ready = (
            sem(n) for n in ("x_ready", "xsq_ready", "xps_used", "ssx_ready", "invx_ready", "xres_ready", "x1_ready"))
        y_ready, y_turned, y_evac, z_ready, z_used = (
            sem(n) for n in ("y_ready", "y_turned", "y_evac", "z_ready", "z_used"))
        below_ready, exp_ready, hot_ready, place_ready, gate_col_ready, res_ready = (
            sem(n) for n in ("below_ready", "exp_ready", "hot_ready", "place_ready", "gate_col_ready", "res_ready"))

        block = ctx.enter_context(nc.Block())

        def half(h):
            return slice(h * HJ, (h + 1) * HJ)

        def rows(bank):
            return bank.rearrange("p (j h) -> p j h", h=H)

        LAGS = 6

        def run(stage, b, *h):
            if 0 <= b < NB:
                stage(b, *h)

        @block.sync
        def _(sp):
            sp.dma_start(c_sb[:, :], c).then_inc(c_in, 16)
            sp.dma_start(wmod_sb[:, :], wmod).then_inc(wmod_in, 16)
            sp.dma_start(xin[:, 0], x_rows[0]).then_inc(x_in[0], 16)
            sp.dma_start(q_w[:, :, :], q_weight.rearrange("(k p) h -> p k h", p=P)).then_inc(qw_in, 16)
            for b in range(1, NB):
                sp.dma_start(xin[:, b], x_rows[b]).then_inc(x_in[b], 16)
            for n in range(U):
                b, h = n // 2, n % 2
                sp.wait_ge(res_ready, n + 1)
                sp.dma_start(out_rows[b][:, half(h), :], res[:, b % 2, half(h), :]).then_inc(out_done[b], 16)
            for b in range(NB):
                sp.wait_ge(out_done[b], 32)

        @block.gpsimd
        def _(pool):
            step = [0]

            def link(ins):
                step[0] += 1
                ins.then_inc(pool_step, 1)
                pool.wait_ge(pool_step, step[0])

            def inv_root(dst, src, ready, count, signal):
                pool.wait_ge(ready, count)
                pool.tensor_tensor(dst, src, minus_half[:, 0:src.shape[1]], ALU.pow).then_inc(signal, 1)

            pool.memset(ident[:, :], 0.0).then_inc(pool_const, 1)
            pool.memset(minus_half[:, :], -0.5).then_inc(pool_const, 1)
            pool.wait_ge(pool_const, 2)
            pool.affine_select(out=ident[:, :], in_=ident[:, :], compare_op=ALU.not_equal, fill=1.0,
                               base=0, pattern=[[-1, P]], channel_multiplier=1).then_inc(pool_const, 1)

            def masks():
                pool.memset(ones[:, :], 1.0).then_inc(pool_const, 1)
                for e in range(E):
                    pool.memset(rank[:, e:e + 1], float(E - e)).then_inc(pool_const, 1)
                pool.wait_ge(pool_const, 4 + E)
                pool.affine_select(out=tri_incl[:, :], in_=ones[:, :], compare_op=ALU.is_ge, fill=0.0,
                                   base=0, pattern=[[1, P]], channel_multiplier=-1).then_inc(pool_const, 1)
                pool.affine_select(out=tri_strict[:, :], in_=ones[:, :], compare_op=ALU.is_gt, fill=0.0,
                                   base=0, pattern=[[1, P]], channel_multiplier=-1).then_inc(pool_const, 1)

            def p1(b, h):
                u = 2 * b + h
                inv_root(rs[:, 0, h, 1], rs[:, 0, h, 0], var_ready[0], u + 1, inv_ready[0])

            def p2(b, h):
                u = 2 * b + h
                pool.wait_ge(mod_rows, 1 if b == 0 else 2)
                pool.wait_ge(norm1_ready, u + 1)
                if u > 1:
                    pool.wait_ge(norm2_ready, u - 1)
                link(pool.tensor_tensor(yh[:, h], ya[:, h], mod_row[:, b, 1:2, :].to_broadcast([P, HJ, H]), ALU.mult))
                pool.tensor_tensor(yh[:, h], yh[:, h], mod_row[:, b, 0:1, :].to_broadcast([P, HJ, H]),
                                   ALU.add).then_inc(h_ready, 1)

            def p3(b, h):
                u = 2 * b + h
                inv_root(rs[:, 1, h, 1], rs[:, 1, h, 0], var_ready[1], u + 1, inv_ready[1])

            def p4(b, h):
                u = 2 * b + h
                if u == 0:
                    pool.wait_ge(ln_in, 32)
                pool.wait_ge(norm2_ready, u + 1)
                link(pool.tensor_tensor(yg[:, h], yg[:, h], lnw[:, :].unsqueeze(1).to_broadcast([P, HJ, H]), ALU.mult))
                link(pool.tensor_tensor(yg[:, h], yg[:, h], lnb[:, :].unsqueeze(1).to_broadcast([P, HJ, H]), ALU.add))
                if u > 1:
                    pool.wait_ge(ssq_ready, u - 1)
                pool.tensor_tensor(gsq[:, h], yg[:, h], yg[:, h], ALU.mult).then_inc(g_ready, 1)

            def p5(b, h):
                u = 2 * b + h
                inv_root(rs[:, 3, h, 1], rs[:, 3, h, 0], ssq_ready, u + 1, invq_ready)

            def p6(b, h):
                u = 2 * b + h
                if u == 0:
                    pool.wait_ge(gate_bias_ready, 1)
                if u > 1:
                    pool.wait_ge(x1_ready, u - 1)
                pool.wait_ge(x_in[b], 16)
                pool.tensor_tensor(xres[:, h], xin[:, b, half(h), :], gate_bias[:, b:b + 1, :].to_broadcast([P, HJ, H]),
                                   ALU.add).then_inc(xres_ready, 1)

            def p7(b, h):
                u = 2 * b + h
                inv_root(rs[:, 4, h, 1], rs[:, 4, h, 0], ssx_ready, u + 1, invx_ready)

            def p8(b, h):
                u = 2 * b + h
                inv_root(rs[:, 2, h, 1], rs[:, 2, h, 0], var_ready[2], u + 1, inv_ready[2])

            def r3(b):
                if b == NB - 1:
                    return
                pool.wait_ge(gate_col_ready, b + 1)
                if b > 1:
                    pool.wait_ge(out_done[b - 2], 32)
                for h in range(2):
                    s = half(h)
                    link(pool.tensor_tensor(res[:, b % 2, s, :], z_sb[:, b % 2, s, :],
                                            keep_gate[:, b % 2, s].unsqueeze(2).to_broadcast([P, HJ, H]), ALU.mult))
                    pool.tensor_tensor(res[:, b % 2, s, :], res[:, b % 2, s, :], x1[:, b % 2, s, :],
                                       ALU.add).then_inc(res_ready, 1)

            def keys():
                pool.wait_ge(k_in, 16)
                pool.tensor_tensor(k_sq[:, :, :], k_sb[:, :, :], k_sb[:, :, :], ALU.mult).then_inc(k_squared, 1)

            def keys_inv():
                inv_root(k_ss[:, 2, :], k_ss[:, 1, :], k_summed, 1, k_inv)

            for b in range(NB + LAGS):
                run(p2, b - 2, 1)
                run(p3, b - 2, 0)
                if b == 2:
                    keys_inv()
                run(p8, b - 5, 1)
                run(p4, b - 2, 0)
                run(p3, b - 2, 1)
                run(p5, b - 2, 0)
                run(r3, b - 6)
                run(p4, b - 2, 1)
                run(p7, b - 4, 0)
                run(p6, b - 4, 1)
                run(p1, b - 1, 0)
                run(p5, b - 2, 1)
                if b == 3:
                    masks()
                if b == 1:
                    keys()
                run(p6, b - 3, 0)
                run(p8, b - 4, 0)
                run(p1, b - 1, 1)
                run(p2, b - 1, 0)
                run(p7, b - 4, 1)

        @block.scalar
        def _(act):
            act.dma_start(k_sb[:, :, :], k_weight.rearrange("(k p) h -> p k h", p=P)).then_inc(k_in, 16)
            act.dma_start(lnw[:, :], ln_weight.partition_broadcast(P)).then_inc(ln_in, 16)
            act.dma_start(lnb[:, :], ln_bias.partition_broadcast(P)).then_inc(ln_in, 16)
            act.preload_act_table_set(LN_EXP)
            act.wait_ge(c_in, 16)
            act.activation(c_tmp[:, 0, :], c_sb[:, :], ACT.Exp, scale=-1.0).then_inc(silu_exp, 1)
            act.dma_start(bias_b[:, :], bias.partition_broadcast(P)).then_inc(rows_in, 16)
            act.dma_start(be_b[:, :], be.partition_broadcast(P)).then_inc(rows_in, 16)
            act.dma_start(wer[:, 0:H], we).then_inc(w_in, 16)
            act.dma_start(wer[:, H:W], wg).then_inc(w_in, 16)
            for n, bs in enumerate((slice(0, 1), slice(1, NB))):
                act.wait_ge(mod_ps, n + 1)
                act.activation(mod_row[:, bs, 1, :], score[:, bs, H:2 * H], ACT.Identity, bias=1.0)
                act.activation(mod_row[:, bs, 0, :], score[:, bs, 0:H], ACT.Copy).then_inc(mod_rows, 1)
            act.activation(mod_row[:, :, 2:4, :], score[:, :, 2 * H:4 * H].rearrange("p b (g h) -> p b g h", h=H),
                           ACT.Copy).then_inc(mod_rows, 1)
            act.activation(gate_t[:, 2], score[:, :, 2 * H:4 * H].rearrange("p b (g h) -> p b g h", h=H),
                           ACT.Abs).then_inc(mod_rows, 1)

            def keys_copy():
                act.wait_ge(k_turned, 1)
                act.activation(k_t[:, :], xps[:, :], ACT.Copy).then_inc(k_ready, 1)

            def e1(b, h):
                u = 2 * b + h
                act.wait_ge(q_turned, u + 1)
                if u > 3:
                    act.wait_ge(score_ready, 2 * (u - 3))
                act.activation(q_t[:, b % 2, h * HT:(h + 1) * HT], turn[:, :], ACT.Copy).then_inc(q_evac, 1)

            def r(b, h, p):
                n = 4 * b + 2 * h + p
                t = root[:, p, :]
                act.wait_ge(score_ready, n + 1)
                if n > 1:
                    act.wait_ge(tan_ready, n - 1)
                act.activation(t.rearrange("p (a t) -> p a t", a=2), score[:, 2 * p:2 * p + 2, :],
                               ACT.Square).then_inc(sq_done, 1)
                act.wait_ge(sq_done, n + 1)
                act.activation(t, t, ACT.Ln, scale=-1.0, bias=1.0).then_inc(ln_done, 1)
                act.wait_ge(ln_done, n + 1)
                act.activation(t, t, ACT.Exp, scale=-0.5).then_inc(root_ready, 1)

            def v(b):
                act.preload_act_table_set(TRIG)
                for h in range(2):
                    t = prob[:, b % 2, h].rearrange("p k t -> p (k t)")
                    act.wait_ge(tan_ready, 4 * b + 2 * h + 2)
                    act.activation(t, t, ACT.Arctan).then_inc(atan_done, 1)
                act.preload_act_table_set(LN_EXP)

            def w(b, h):
                u = 2 * b + h
                t = prob[:, b % 2, h].rearrange("p k t -> p (k t)")
                act.wait_ge(atan_done, u + 1)
                act.activation(t, t, ACT.Ln, scale=1.0 / PI, bias=0.5).then_inc(lnp_done, 1)
                act.wait_ge(lnp_done, u + 1)
                act.activation(t, t, ACT.Exp, scale=TAU).then_inc(prob_ready, 1)

            def xs(b, h):
                u = 2 * b + h
                act.wait_ge(x_ready, u + 1)
                if u > 1:
                    act.wait_ge(ssx_ready, u - 1)
                act.activation(xsq[:, h], rows(xps[:, :]), ACT.Square).then_inc(xsq_ready, 1)

            def e2(b, h):
                u = 2 * b + h
                act.wait_ge(y_turned, u + 1)
                if u > 1:
                    act.wait_ge(z_ready, u - 1)
                act.activation(y_t[:, h], turn[:, :], ACT.Copy).then_inc(y_evac, 1)

            def ex(b):
                act.wait_ge(below_ready, b + 1)
                act.activation(rt[:, 1], rt[:, 0], ACT.Exp).then_inc(exp_ready, 1)

            for b in range(NB + LAGS):
                run(xs, b - 4, 1)
                run(w, b - 3, 0)
                run(r, b - 2, 0, 0)
                run(e1, b - 2, 1)
                run(r, b - 2, 0, 1)
                run(ex, b - 5)
                run(r, b - 2, 1, 0)
                run(e2, b - 4, 0)
                run(r, b - 2, 1, 1)
                run(w, b - 3, 1)
                run(xs, b - 3, 0)
                run(e2, b - 4, 1)
                run(v, b - 2)
                run(e1, b - 1, 0)
                if b == 0:
                    keys_copy()

        @block.vector
        def _(dve):
            step = [0]

            def link(ins):
                step[0] += 1
                ins.then_inc(dve_step, 1)
                dve.wait_ge(dve_step, step[0])

            def stats(src, i, h, eps):
                for j in range(HJ):
                    last = dve.bn_stats(bn[:, i, j, :], src[:, j, :])
                link(last)
                for j in range(HJ):
                    last = dve.bn_aggr(st[:, i, h, j, :], bn[:, i, j, :])
                link(last)
                dve.tensor_scalar(rs[:, i, h, 0], st[:, i, h, :, 1], eps, None, ALU.add).then_inc(var_ready[i], 1)

            def normed(dst, src, i, h, signal):
                for j in range(HJ):
                    last = dve.tensor_scalar(dst[:, j, :], src[:, j, :], st[:, i, h, j, 0:1], rs[:, i, h, 1, j:j + 1],
                                             ALU.subtract, ALU.mult)
                last.then_inc(signal, 1)

            def a1(b, h):
                dve.wait_ge(x_in[b], 16)
                u = 2 * b + h
                if u > 1:
                    dve.wait_ge(norm1_ready, u - 1)
                stats(xin[:, b, half(h), :], 0, h, 1e-5)

            def a2(b, h):
                u = 2 * b + h
                dve.wait_ge(inv_ready[0], u + 1)
                if u > 1:
                    dve.wait_ge(h_ready, u - 1)
                normed(ya[:, h], xin[:, b, half(h), :], 0, h, norm1_ready)

            def a3(b, h):
                dve.wait_ge(h_ready, 2 * b + h + 1)
                stats(yh[:, h], 1, h, 1e-12)

            def a4(b, h):
                u = 2 * b + h
                dve.wait_ge(inv_ready[1], u + 1)
                if u > 1:
                    dve.wait_ge(q_ready, u - 1)
                normed(yg[:, h], yh[:, h], 1, h, norm2_ready)

            def a5(b, h):
                dve.wait_ge(g_ready, 2 * b + h + 1)
                link(dve.tensor_reduce(ss[:, 0, :], gsq[:, h], AX.X, ALU.add))
                dve.tensor_scalar(rs[:, 3, h, 0], ss[:, 0, :], 1e-24, None, ALU.max).then_inc(ssq_ready, 1)

            def a6(b, h):
                u = 2 * b + h
                dve.wait_ge(invq_ready, u + 1)
                if u > 1:
                    dve.wait_ge(q_turned, u - 1)
                dve.tensor_tensor(yq[:, h], yg[:, h], rs[:, 3, h, 1].unsqueeze(2).to_broadcast([P, HJ, H]),
                                  ALU.mult).then_inc(q_ready, 1)

            def g(b, h, p):
                n = 4 * b + 2 * h + p
                dve.wait_ge(root_ready, n + 1)
                if b > 1:
                    dve.wait_ge(x_ready, 2 * (b - 2) + h + 1)
                dve.scalar_tensor_tensor(out=prob[:, b % 2, h, 2 * p:2 * p + 2, :],
                                         in0=root[:, p, :].rearrange("p (a t) -> p a t", a=2), scalar=TAN_MAX,
                                         in1=score[:, 2 * p:2 * p + 2, :],
                                         op0=ALU.min, op1=ALU.mult).then_inc(tan_ready, 1)

            def xe(b, h):
                u = 2 * b + h
                if u == 0:
                    dve.wait_ge(gate_ready, 1)
                dve.wait_ge(xsq_ready, u + 1)
                if u > 1:
                    dve.wait_ge(x1_ready, u - 1)
                dve.tensor_tensor(xa[:, h], rows(xps[:, :]), gates[:, b, 0:1, :].to_broadcast([P, HJ, H]),
                                  ALU.mult).then_inc(xps_used, 1)

            def c1(b, h):
                dve.wait_ge(xsq_ready, 2 * b + h + 1)
                link(dve.tensor_reduce(ss[:, 1, :], xsq[:, h], AX.X, ALU.add))
                dve.tensor_scalar(rs[:, 4, h, 0], ss[:, 1, :], 1e-24, None, ALU.max).then_inc(ssx_ready, 1)

            def c2(b, h):
                u = 2 * b + h
                dve.wait_ge(invx_ready, u + 1)
                dve.wait_ge(xres_ready, u + 1)
                dve.wait_ge(xps_used, u + 1)
                if b > 1:
                    dve.wait_ge(res_ready, 2 * (b - 2) + h + 1)
                for j in range(HJ):
                    last = dve.scalar_tensor_tensor(out=x1[:, b % 2, h * HJ + j, :], in0=xa[:, h, j, :],
                                                    scalar=rs[:, 4, h, 1, j:j + 1], in1=xres[:, h, j, :],
                                                    op0=ALU.mult, op1=ALU.add)
                last.then_inc(x1_ready, 1)

            def c3(b, h):
                dve.wait_ge(x1_ready, 2 * b + h + 1)
                stats(x1[:, b % 2, half(h), :], 2, h, 1e-5)

            def c4(b, h):
                u = 2 * b + h
                dve.wait_ge(inv_ready[2], u + 1)
                if u > 1:
                    dve.wait_ge(y_turned, u - 1)
                normed(yc[:, h], x1[:, b % 2, half(h), :], 2, h, y_ready)

            def ze(b, h):
                u = 2 * b + h
                dve.wait_ge(z_ready, u + 1)
                if b > 1:
                    dve.wait_ge(res_ready, 2 * (b - 1))
                for i in range(2):
                    t = slice(h * HJ + 2 * i, h * HJ + 2 * i + 2)
                    dve.tensor_tensor(logit[:, b % 2, t, :], zview[:, i, :, H:W],
                                      const_b[:, b:b + 1, H:W].to_broadcast([P, 2, E]), ALU.add)
                    last = dve.tensor_tensor(z_sb[:, b % 2, t, :], zview[:, i, :, 0:H],
                                             const_b[:, b:b + 1, 0:H].to_broadcast([P, 2, H]), ALU.add)
                last.then_inc(z_used, 1)

            def wide(col):
                return col.unsqueeze(2).to_broadcast([P, J, E])

            def r1(b):
                lg = logit[:, b % 2]
                dve.wait_ge(z_used, 2 * b + 2)
                link(dve.tensor_reduce(rc[:, 0, :], lg, AX.X, ALU.max))
                link(dve.tensor_tensor(rt[:, 2], lg, wide(rc[:, 0, :]), ALU.is_equal))
                link(dve.tensor_tensor(rt[:, 3], rt[:, 2], rank[:, :].unsqueeze(1).to_broadcast([P, J, E]), ALU.mult))
                link(dve.tensor_reduce(rc[:, 1, :], rt[:, 3], AX.X, ALU.max))
                link(dve.tensor_tensor(hot[:, :, :], rt[:, 3], wide(rc[:, 1, :]), ALU.is_equal))
                dve.tensor_tensor(rt[:, 0], lg, wide(rc[:, 0, :]), ALU.subtract).then_inc(below_ready, 1)
                link(dve.tensor_reduce(rt[:, 4, 0, :], hot[:, :, :].rearrange("p j e -> p e j"), AX.X, ALU.add))
                dve.tensor_tensor(taken[:, (b + 1) % 2, :], taken[:, b % 2, :], rt[:, 4, 0, :], ALU.add).then_inc(hot_ready, 1)

            def r2(b):
                dve.wait_ge(exp_ready, b + 1)
                link(dve.tensor_reduce(rc[:, 2, :], rt[:, 1], AX.X, ALU.add))
                dve.reciprocal(rc[:, 3, :], rc[:, 2, :])
                dve.wait_ge(place_ready, b + 1)
                link(dve.scalar_tensor_tensor(out=rt[:, 5], in0=place, scalar=CAP, in1=hot[:, :, :],
                                              op0=ALU.is_le, op1=ALU.mult))
                link(dve.tensor_reduce(rc[:, 4, :], rt[:, 5], AX.X, ALU.add))
                dve.tensor_tensor(keep_gate[:, b % 2, :], rc[:, 4, :], rc[:, 3, :], ALU.mult).then_inc(gate_col_ready, 1)

            def r3(b):
                if b < NB - 1:
                    return
                dve.wait_ge(gate_col_ready, b + 1)
                dve.wait_ge(out_done[b - 2], 32)
                for h in range(2):
                    if h == 0:
                        dve.wait_ge(res_ready, 2 * b)
                    for j in range(h * HJ, (h + 1) * HJ):
                        last = dve.scalar_tensor_tensor(out=res[:, b % 2, j, :], in0=z_sb[:, b % 2, j, :],
                                                        scalar=keep_gate[:, b % 2, j:j + 1], in1=x1[:, b % 2, j, :],
                                                        op0=ALU.mult, op1=ALU.add)
                    last.then_inc(res_ready, 1)

            def silu():
                dve.wait_ge(silu_exp, 1)
                link(dve.tensor_scalar(c_tmp[:, 1, :], c_tmp[:, 0, :], 1.0, None, ALU.add))
                link(dve.reciprocal(c_tmp[:, 2, :], c_tmp[:, 1, :]))
                dve.tensor_tensor(c_silu[:, :], c_sb[:, :], c_tmp[:, 2, :], ALU.mult).then_inc(silu_row, 1)
                dve.wait_ge(silu_turn, 1)
                dve.tensor_copy(silu_t[:, :], turn[:, 0:NB]).then_inc(silu_col, 1)
                dve.tensor_copy(silu_b[:, :, :], turn[:, 0:NB].unsqueeze(2).to_broadcast([P, NB, P])).then_inc(silu_wide, 1)

            def keys_sum():
                dve.wait_ge(k_squared, 1)
                link(dve.tensor_reduce(k_ss[:, 0, :], k_sq[:, :, :], AX.X, ALU.add))
                dve.tensor_scalar(k_ss[:, 1, :], k_ss[:, 0, :], 1e-24, None, ALU.max).then_inc(k_summed, 1)

            def keys_scale():
                dve.wait_ge(k_inv, 1)
                dve.tensor_tensor(k_unit[:, :, :], k_sb[:, :, :], k_ss[:, 2, :].unsqueeze(2).to_broadcast([P, KC, H]),
                                  ALU.mult).then_inc(k_scaled, 1)

            def mod_columns():
                dve.wait_ge(mod_cols, 1)
                dve.tensor_copy(modc[:, 0, :], turn[:, 0:NB])
                dve.tensor_scalar(modc[:, 1, :], turn[:, NB:2 * NB], 1.0, None, ALU.add).then_inc(modc_ready, 1)

            def gate_rows():
                dve.wait_ge(mod_rows, 4)
                gr = mod_row[:, :, 2:4, :]
                two, sign, size = (gate_t[:, i] for i in range(3))
                link(dve.tensor_scalar(two, gr, 0.0, 2.0, ALU.is_ge, ALU.mult))
                link(dve.tensor_scalar(sign, two, -1.0, None, ALU.add))
                flat = [t.rearrange("p b g h -> p (b g h)") for t in (gates[:, :, :, :], size, sign)]
                dve.scalar_tensor_tensor(out=flat[0], in0=flat[1], scalar=0.25, in1=flat[2],
                                         op0=ALU.max, op1=ALU.mult).then_inc(gate_ready, 1)
                dve.wait_ge(gate_ready, 1)
                dve.wait_ge(rows_in, 32)
                dve.tensor_tensor(gate_bias[:, :, :], gates[:, :, 0, :],
                                  bias_b[:, :].unsqueeze(1).to_broadcast([P, NB, H]), ALU.mult).then_inc(gate_bias_ready, 1)

            def fold_weights():
                dve.wait_ge(modc_ready, 1)
                dve.tensor_copy(shift2_b[:, :, :], modc[:, 0, :].unsqueeze(2).to_broadcast([P, NB, P])).then_inc(shift2_ready, 1)
                dve.wait_ge(w_in, 32)
                for b in range(NB):
                    dve.scalar_tensor_tensor(out=wer_b[:, b, 0:H], in0=wer[:, 0:H], scalar=modc[:, 1, b:b + 1],
                                             in1=gates[:, b, 1, :], op0=ALU.mult, op1=ALU.mult)
                    last = dve.tensor_scalar(wer_b[:, b, H:W], wer[:, H:W], modc[:, 1, b:b + 1], None, ALU.mult)
                last.then_inc(wer_ready, 1)

            def fold_constants():
                dve.wait_ge(const_ps, 1)
                for i in range(2):
                    dve.tensor_tensor(const_b[:, 2 * i:2 * i + 2, 0:H], zview[:, i, :, 0:H],
                                      be_b[:, :].unsqueeze(1).to_broadcast([P, 2, H]), ALU.add)
                    last = dve.tensor_copy(const_b[:, 2 * i:2 * i + 2, H:W], zview[:, i, :, H:W])
                link(last)
                dve.tensor_tensor(const_b[:, :, 0:H], const_b[:, :, 0:H], gates[:, :, 1, :], ALU.mult).then_inc(const_ready, 1)

            dve.memset(taken[:, :, :], 0.0)
            silu()
            for b in range(NB + LAGS):
                run(c3, b - 5, 1)
                run(a4, b - 2, 0)
                run(r2, b - 6)
                if b == 2:
                    keys_scale()
                run(a3, b - 2, 1)
                if b == 2:
                    mod_columns()
                run(c4, b - 5, 1)
                run(g, b - 3, 1, 0)
                run(g, b - 3, 1, 1)
                run(a5, b - 2, 0)
                run(a4, b - 2, 1)
                run(ze, b - 5, 0)
                run(xe, b - 4, 0)
                run(c1, b - 4, 0)
                run(ze, b - 5, 1)
                run(a6, b - 2, 0)
                run(r3, b - 6)
                if b == 3:
                    gate_rows()
                run(r1, b - 5)
                if b == 4:
                    fold_constants()
                run(a1, b - 1, 1)
                run(a5, b - 2, 1)
                run(a2, b - 1, 0)
                if b == 1:
                    keys_sum()
                run(c2, b - 4, 0)
                run(c3, b - 4, 0)
                run(a6, b - 2, 1)
                run(c1, b - 4, 1)
                run(xe, b - 4, 1)
                if b == 3:
                    fold_weights()
                run(c4, b - 4, 0)
                run(a2, b - 1, 1)
                run(g, b - 2, 0, 0)
                run(c2, b - 4, 1)
                run(a3, b - 1, 0)
                run(g, b - 2, 0, 1)
                run(a1, b, 0)

        @block.tensor
        def _(pe):
            pe.wait_ge(silu_row, 1)
            pe.wait_ge(pool_const, 3)
            pe.transpose(turn[:, 0:NB], c_silu[:, :], ident[0:NB, 0:NB]).then_inc(silu_turn, 1)
            pe.wait_ge(silu_wide, 1)
            pe.wait_ge(wmod_in, 16)
            for b in range(NB):
                pe.matmul(score[:, b, 0:3 * H], silu_b[:, b, :], wmod_sb[:, 0:3 * H], start=True, stop=True)
                last = pe.matmul(score[:, b, 3 * H:4 * H], silu_b[:, b, :], wmod_sb[:, 5 * H:6 * H], start=True, stop=True)
                if b in (0, NB - 1):
                    last.then_inc(mod_ps, 1)
            for i in range(2):
                last = pe.matmul(turn[:, i * NB:(i + 1) * NB], wmod_sb[:, (3 + i) * H:(4 + i) * H], silu_t[:, :],
                                 start=True, stop=True)
            last.then_inc(mod_cols, 1)

            def keys_turn():
                pe.wait_ge(k_scaled, 1)
                for k in range(KC):
                    last = pe.transpose(xps[:, k * P:(k + 1) * P], k_unit[:, k, :], ident[:, :])
                last.then_inc(k_turned, 1)

            turns = [0, 0]

            def bank_free():
                if turns[0]:
                    pe.wait_ge(q_evac, turns[0])
                else:
                    pe.wait_ge(modc_ready, 1)
                if turns[1]:
                    pe.wait_ge(y_evac, turns[1])

            def t1(b, h):
                pe.wait_ge(q_ready, 2 * b + h + 1)
                bank_free()
                for j in range(HJ):
                    last = pe.transpose(turn[:, j * P:(j + 1) * P], yq[:, h, j, :], ident[:, :])
                last.then_inc(q_turned, 1)
                turns[0] += 1

            def s(b, h, p):
                n = 4 * b + 2 * h + p
                pe.wait_ge(q_evac, 2 * b + h + 1)
                if n == 0:
                    pe.wait_ge(k_ready, 1)
                    pe.wait_ge(mod_rows, 4)
                if n > 1:
                    pe.wait_ge(tan_ready, n - 1)
                for i in range(2):
                    k = 2 * p + i
                    last = pe.matmul(score[:, 2 * p + i, :], k_t[:, k * P:(k + 1) * P],
                                     q_t[:, b % 2, h * HT:(h + 1) * HT], start=True, stop=True)
                last.then_inc(score_ready, 1)

            def x(b, h):
                u = 2 * b + h
                pe.wait_ge(prob_ready, u + 1)
                if u == 0:
                    pe.wait_ge(qw_in, 16)
                else:
                    pe.wait_ge(xps_used, u)
                for j in range(HJ):
                    for k in range(KC):
                        last = pe.matmul(xps[:, j * H:(j + 1) * H], prob[:, b % 2, h, k, j * P:(j + 1) * P],
                                         q_w[:, k, :], start=(k == 0), stop=(k == KC - 1))
                last.then_inc(x_ready, 1)

            def t2(b, h):
                pe.wait_ge(y_ready, 2 * b + h + 1)
                bank_free()
                for j in range(HJ):
                    last = pe.transpose(turn[:, j * P:(j + 1) * P], yc[:, h, j, :], ident[:, :])
                last.then_inc(y_turned, 1)
                turns[1] += 1

            projected = [0]
            queued = [0]

            def z(b, h):
                u = 2 * b + h
                pe.wait_ge(y_evac, u + 1)
                if u == 0:
                    pe.wait_ge(const_ready, 1)
                    pe.wait_ge(wer_ready, 1)
                else:
                    pe.wait_ge(z_used, u)
                if queued[0]:
                    pe.wait_ge(gate_col_ready, queued[0])
                for j in range(HJ):
                    last = pe.matmul(zview[:, j // 2, j % 2, :], y_t[:, h, j * P:(j + 1) * P],
                                     wer_b[:, b, :], start=True, stop=True)
                last.then_inc(z_ready, 1)
                projected[0] = u + 1

            def q(b):
                pe.wait_ge(hot_ready, b + 1)
                if b == 0:
                    pe.wait_ge(pool_const, 6 + E)
                pe.wait_ge(z_used, projected[0])
                if b > 0:
                    pe.wait_ge(gate_col_ready, b)
                queued[0] = b + 1
                pe.matmul(place, ones[:, :], taken[:, b % 2, :].unsqueeze(1).to_broadcast([P, J, E]),
                          start=True, stop=False)
                for j in range(J):
                    if j > 0:
                        pe.matmul(place[:, 0:j, :], tri_strict[:, :], hot[:, j:j + 1, :].to_broadcast([P, j, E]),
                                  start=False, stop=False)
                    last = pe.matmul(place[:, j:J, :], tri_incl[:, :], hot[:, j:j + 1, :].to_broadcast([P, J - j, E]),
                                     start=False, stop=(j == J - 1))
                last.then_inc(place_ready, 1)

            def constants():
                pe.wait_ge(shift2_ready, 1)
                pe.wait_ge(w_in, 32)
                for b in range(NB):
                    last = pe.matmul(zview[:, b // 2, b % 2, :], shift2_b[:, b, :], wer[:, :], start=True, stop=True)
                last.then_inc(const_ps, 1)

            for b in range(NB + LAGS):
                run(x, b - 4, 0)
                run(z, b - 5, 0)
                run(t2, b - 5, 1)
                run(z, b - 5, 1)
                run(x, b - 4, 1)
                run(t1, b - 2, 0)
                run(q, b - 5)
                run(s, b - 2, 0, 0)
                run(s, b - 2, 0, 1)
                run(t1, b - 2, 1)
                if b == 1:
                    keys_turn()
                run(t2, b - 4, 0)
                if b == 3:
                    constants()
                run(s, b - 2, 1, 0)
                run(s, b - 2, 1, 1)


_INS = ["L0_attn_hidden_states", "L0_attn_ln_weight", "L0_attn_ln_bias", "L0_attn_k_weight", "L0_attn_q_weight",
        "L0_attn_bias", "L0_ffn_Wg", "L0_ffn_We", "L0_ffn_be", "L0_c", "L0_wmod"]


def kernel(**inputs):
    import numpy as _np
    import concourse.bacc as _bacc
    from concourse import mybir as _mybir
    from concourse.bass_utils import run_bass_kernel_spmd as _run

    nc = _bacc.Bacc("TRN2", target_bir_lowering=False, num_devices=1)
    arrays, args = {}, []
    for name in _INS:
        a = _np.ascontiguousarray(inputs[name])
        arrays[f"in_{name}_dram"] = a
        args.append(nc.dram_tensor(f"in_{name}_dram", a.shape, _mybir.dt.from_np(a.dtype), kind="ExternalInput").ap())
    shape = inputs["L0_attn_hidden_states"].shape
    out = nc.dram_tensor("out_0_dram", tuple(shape), _mybir.dt.from_np(_np.dtype("float32")), kind="ExternalOutput").ap()
    adaln_block(nc, *args, out)
    r = _run(nc, [arrays], core_ids=[0])
    return r.results[0]["out_0_dram"]
```

```python
from contextlib import ExitStack

import concourse.bass as bass
from concourse import mybir

F32 = mybir.dt.float32
BF16 = mybir.dt.bfloat16
ALU = mybir.AluOpType
ACT = mybir.ActivationFunctionType
AX = mybir.AxisListType

P = 128
H = 128
PI = 3.141592653589793
CLIP = 1.0 - 1e-6
TAN_MAX = (1.0 - CLIP * CLIP) ** -0.5
TAU = 9.0
LN_EXP = "natural_log_exp_and_others"
TRIG = "trig_and_small"


def adaln_block(nc, x, c_t, rows4, k_weight, q_weight, weg, wmod, out):
    NB, T, _ = x.shape
    J = T // P
    HJ = J // 2
    HT = T // 2
    KEYS = k_weight.shape[0]
    KC = KEYS // P
    E = weg.shape[1] - H
    CAP = float(NB * T // E)
    W = H + E
    U = 2 * NB

    x_rows = x.rearrange("b (p j) h -> b p j h", p=P)
    out_rows = out.rearrange("b (p j) h -> b p j h", p=P)

    with ExitStack() as ctx:
        def sb(name, shape, dt=F32):
            return ctx.enter_context(nc.sbuf_tensor(name, shape, dt))

        def sem(name):
            return ctx.enter_context(nc.semaphore(name))

        score = ctx.enter_context(nc.psum_tensor("score", [P, 4, 512], F32))
        turn = ctx.enter_context(nc.psum_tensor("turn", [P, 512], F32))
        xps = ctx.enter_context(nc.psum_tensor("xps", [P, 512], F32))
        zps = ctx.enter_context(nc.psum_tensor("zps", [P, 2, 512], F32))
        zview = zps[:, :, 0:2 * W].rearrange("p a (t w) -> p a t w", t=2)
        place = zps[:, 0, 384:384 + J * E].rearrange("p (j e) -> p j e", e=E)

        ident = sb("ident", [P, P])
        tri_incl = sb("tri_incl", [P, P], BF16)
        tri_strict = sb("tri_strict", [P, P], BF16)
        ones = sb("ones", [P, P], BF16)
        minus_half = sb("minus_half", [P, J])
        rank = sb("rank", [P, E])
        c_sb = sb("c_sb", [P, NB])
        c_tmp = sb("c_tmp", [P, 3, NB])
        silu_t = sb("silu_t", [P, NB])
        silu_b = sb("silu_b", [P, NB, P])
        wmod_sb = sb("wmod_sb", [P, 6 * H])
        mod_row = sb("mod_row", [P, NB, 4, H])
        gates = sb("gates", [P, NB, 2, H])
        gate_t = sb("gate_t", [P, 3, NB, 2, H])
        gate_bias = sb("gate_bias", [P, NB, H])
        modc = sb("modc", [P, 2, NB])
        shift2_b = sb("shift2_b", [P, NB, P])
        rows_b = sb("rows_b", [P, 4, H])
        lnw, lnb, bias_b, be_b = (rows_b[:, i, :] for i in range(4))
        wer = sb("wer", [P, W])
        wer_b = sb("wer_b", [P, NB, W])
        const_b = sb("const_b", [P, NB, W])
        k_sb = sb("k_sb", [P, KC, H])
        k_sq = sb("k_sq", [P, KC, H])
        k_unit = sb("k_unit", [P, KC, H])
        k_ss = sb("k_ss", [P, 2, KC])
        k_t = sb("k_t", [P, KEYS])
        q_w = sb("q_w", [P, KC, H])

        xin = sb("xin", [P, NB, J, H])
        ya = sb("ya", [P, 2, HJ, H])
        yh = sb("yh", [P, 2, HJ, H])
        yg = sb("yg", [P, 2, HJ, H])
        gsq = sb("gsq", [P, 2, HJ, H])
        yq = sb("yq", [P, 2, HJ, H])
        bn = sb("bn", [P, 3, 2, HJ, 6])
        st = sb("st", [P, 3, 2, HJ, 2])
        ss = sb("ss", [P, 2, 2, HJ])
        rs = sb("rs", [P, 5, 2, HJ])
        q_t = sb("q_t", [P, 2, T])
        root = sb("root", [P, 2, 1024])
        prob = sb("prob", [P, 2, 2, KC, HT])
        xsq = sb("xsq", [P, 2, HJ, H])
        xa = sb("xa", [P, 2, HJ, H])
        xres = sb("xres", [P, 2, HJ, H])
        x1 = sb("x1", [P, 2, J, H])
        yc = sb("yc", [P, 2, HJ, H])
        y_t = sb("y_t", [P, 2, HT])
        z_sb = sb("z_sb", [P, 2, J, H])
        logit = sb("logit", [P, 2, J, E])
        rt = sb("rt", [P, 6, J, E])
        rc = sb("rc", [P, 6, J])
        keep_gate = sb("keep_gate", [P, 2, J])
        hot = sb("hot", [P, J, E], BF16)
        taken = sb("taken", [P, 2, E], BF16)
        res = sb("res", [P, 2, J, H])

        x_in = [sem(f"x_in{b}") for b in range(NB)]
        c_in, wmod_first_in, wmod_in, k_in, qw_in, w_in, rows_in = (
            sem(n) for n in ("c_in", "wmod_first_in", "wmod_in", "k_in", "qw_in", "w_in", "rows_in"))
        out_done = [sem(f"out_done{b}") for b in range(NB)]
        pool_const = sem("pool_const")
        dve_step = sem("dve_step")
        pool_step = sem("pool_step")
        silu_exp, silu_wide = sem("silu_exp"), sem("silu_wide")
        mod_ps, mod_cols, mod_rows, gate_ready, gate_bias_ready, modc_ready, shift2_ready = (
            sem(n) for n in ("mod_ps", "mod_cols", "mod_rows", "gate_ready", "gate_bias_ready", "modc_ready",
                             "shift2_ready"))
        wer_ready, const_ps, const_ready = (sem(n) for n in ("wer_ready", "const_ps", "const_ready"))
        k_summed, k_inv, k_scaled, k_turned, k_ready = (
            sem(n) for n in ("k_summed", "k_inv", "k_scaled", "k_turned", "k_ready"))
        var_ready = [sem(f"var{i}_ready") for i in range(3)]
        inv_ready = [sem(f"inv{i}_ready") for i in range(3)]
        norm1_ready, h_ready, norm2_ready, g_ready, ssq_ready, invq_ready = (
            sem(n) for n in ("norm1_ready", "h_ready", "norm2_ready", "g_ready", "ssq_ready", "invq_ready"))
        q_ready, q_turned, q_evac = (sem(n) for n in ("q_ready", "q_turned", "q_evac"))
        score_ready, sq_done, ln_done, root_ready, tan_ready = (
            sem(n) for n in ("score_ready", "sq_done", "ln_done", "root_ready", "tan_ready"))
        atan_done, lnp_done, prob_ready = (sem(n) for n in ("atan_done", "lnp_done", "prob_ready"))
        x_ready, xps_used, ssx_ready, invx_ready, xres_ready, x1_ready = (
            sem(n) for n in ("x_ready", "xps_used", "ssx_ready", "invx_ready", "xres_ready", "x1_ready"))
        y_ready, y_turned, y_evac, z_ready, z_used = (
            sem(n) for n in ("y_ready", "y_turned", "y_evac", "z_ready", "z_used"))
        below_ready, exp_ready, hot_ready, taken_ready, place_ready, gate_col_ready, res_ready = (
            sem(n) for n in ("below_ready", "exp_ready", "hot_ready", "taken_ready", "place_ready", "gate_col_ready", "res_ready"))

        block = ctx.enter_context(nc.Block())

        def half(h):
            return slice(h * HJ, (h + 1) * HJ)

        def rows(bank):
            return bank.rearrange("p (j h) -> p j h", h=H)

        FAST = 2
        LAGS = 6

        def run(stage, b, *h):
            if 0 <= b < NB and (b == NB - 1 or h[:1] != (2,)):
                stage(b, *h)

        def piece(b, h):
            n = 2 * b + h
            if n < U - 1:
                return n % 2, h * HJ, HJ
            return n % 2, HJ + (h - 1) * HJ // 2, HJ // 2

        def banks(h):
            if h < 2:
                return rows(xps[:, :]), turn[:, :], zview
            return rows(score[:, 0, :]), score[:, 1, :], score[:, 2:3, 0:2 * W].rearrange("p a (t w) -> p a t w", t=2)

        @block.sync
        def _(sp):
            sp.dma_start(c_sb[:, :], c_t).then_inc(c_in, 16)
            sp.dma_start(wmod_sb[:, 0:2 * H], wmod[:, 0:2 * H]).then_inc(wmod_first_in, 16)
            sp.dma_start(xin[:, 0], x_rows[0]).then_inc(x_in[0], 16)
            sp.dma_start(wmod_sb[:, 2 * H:6 * H], wmod[:, 2 * H:6 * H]).then_inc(wmod_in, 16)
            sp.dma_start(rows_b[:, :, :], rows4.partition_broadcast(P)).then_inc(rows_in, 16)
            sp.dma_start(xin[:, 1], x_rows[1]).then_inc(x_in[1], 16)
            sp.dma_start(q_w[:, :, :], q_weight.rearrange("(k p) h -> p k h", p=P)).then_inc(qw_in, 16)
            for b in range(2, NB):
                sp.dma_start(xin[:, b], x_rows[b]).then_inc(x_in[b], 16)
            for n in range(U):
                b, h = n // 2, n % 2
                sp.wait_ge(res_ready, n + 1)
                sp.dma_start(out_rows[b][:, half(h), :], res[:, b % 2, half(h), :]).then_inc(out_done[b], 16)
            for b in range(NB):
                sp.wait_ge(out_done[b], 32)

        @block.gpsimd
        def _(pool):
            step = [0]

            def link(ins):
                step[0] += 1
                ins.then_inc(pool_step, 1)
                pool.wait_ge(pool_step, step[0])

            def inv_root(dst, src, guard, bound, ready, count, signal):
                pool.wait_ge(ready, count)
                link(pool.tensor_scalar(dst, src, bound, None, guard))
                pool.tensor_tensor(dst, dst, minus_half[:, 0:src.shape[1]], ALU.pow).then_inc(signal, 1)

            pool.memset(ident[:, :], 0.0).then_inc(pool_const, 1)
            pool.memset(minus_half[:, :], -0.5).then_inc(pool_const, 1)
            pool.wait_ge(pool_const, 2)
            pool.affine_select(out=ident[:, :], in_=ident[:, :], compare_op=ALU.not_equal, fill=1.0,
                               base=0, pattern=[[-1, P]], channel_multiplier=1).then_inc(pool_const, 1)

            def masks():
                pool.memset(ones[:, :], 1.0).then_inc(pool_const, 1)
                for e in range(E):
                    pool.memset(rank[:, e:e + 1], float(E - e)).then_inc(pool_const, 1)
                pool.wait_ge(pool_const, 4 + E)
                pool.affine_select(out=tri_incl[:, :], in_=ones[:, :], compare_op=ALU.is_ge, fill=0.0,
                                   base=0, pattern=[[1, P]], channel_multiplier=-1).then_inc(pool_const, 1)
                pool.affine_select(out=tri_strict[:, :], in_=ones[:, :], compare_op=ALU.is_gt, fill=0.0,
                                   base=0, pattern=[[1, P]], channel_multiplier=-1).then_inc(pool_const, 1)

            def p1(b, h):
                u = 2 * b + h
                inv_root(rs[:, 0, h], st[:, 0, h, :, 1], ALU.add, 1e-5, var_ready[0], u + 1, inv_ready[0])

            def p2(b, h):
                u = 2 * b + h
                if u < FAST:
                    return
                pool.wait_ge(mod_rows, 2 if b == 0 else 3)
                pool.wait_ge(norm1_ready, u + 1)
                if u > 1:
                    pool.wait_ge(norm2_ready, u - 1)
                link(pool.tensor_tensor(yh[:, h], ya[:, h], mod_row[:, b, 1:2, :].to_broadcast([P, HJ, H]), ALU.mult))
                pool.tensor_tensor(yh[:, h], yh[:, h], mod_row[:, b, 0:1, :].to_broadcast([P, HJ, H]),
                                   ALU.add).then_inc(h_ready, 1)

            def p3(b, h):
                u = 2 * b + h
                inv_root(rs[:, 1, h], st[:, 1, h, :, 1], ALU.add, 1e-12, var_ready[1], u + 1, inv_ready[1])

            def p4(b, h):
                u = 2 * b + h
                if u < FAST:
                    return
                pool.wait_ge(rows_in, 16)
                pool.wait_ge(norm2_ready, u + 1)
                link(pool.tensor_tensor(yg[:, h], yg[:, h], lnw.unsqueeze(1).to_broadcast([P, HJ, H]), ALU.mult))
                pool.tensor_tensor(yg[:, h], yg[:, h], lnb.unsqueeze(1).to_broadcast([P, HJ, H]),
                                   ALU.add).then_inc(g_ready, 1)

            def p5(b, h):
                u = 2 * b + h
                inv_root(rs[:, 3, h], ss[:, 0, h], ALU.max, 1e-24, ssq_ready, u + 1, invq_ready)

            def p6(b, h):
                n = 2 * b + h
                m, j0, nj = piece(b, h)
                if n == 0:
                    pool.wait_ge(gate_bias_ready, 1)
                if n > 1:
                    pool.wait_ge(x1_ready, n - 1)
                pool.wait_ge(x_in[b], 16)
                pool.tensor_tensor(xres[:, m, 0:nj], xin[:, b, j0:j0 + nj, :],
                                   gate_bias[:, b:b + 1, :].to_broadcast([P, nj, H]), ALU.add).then_inc(xres_ready, 1)

            def p7(b, h):
                m, j0, nj = piece(b, h)
                inv_root(rs[:, 4, m, 0:nj], ss[:, 1, m, 0:nj], ALU.max, 1e-24, ssx_ready, 2 * b + h + 1, invx_ready)

            def p8(b, h):
                m, j0, nj = piece(b, h)
                inv_root(rs[:, 2, m, 0:nj], st[:, 2, m, 0:nj, 1], ALU.add, 1e-5, var_ready[2], 2 * b + h + 1, inv_ready[2])

            def r3(b):
                if b == NB - 1:
                    return
                pool.wait_ge(gate_col_ready, b + 1)
                if b > 1:
                    pool.wait_ge(out_done[b - 2], 32)
                for h in range(2):
                    s = half(h)
                    link(pool.tensor_tensor(res[:, b % 2, s, :], z_sb[:, b % 2, s, :],
                                            keep_gate[:, b % 2, s].unsqueeze(2).to_broadcast([P, HJ, H]), ALU.mult))
                    pool.tensor_tensor(res[:, b % 2, s, :], res[:, b % 2, s, :], x1[:, b % 2, s, :],
                                       ALU.add).then_inc(res_ready, 1)

            def keys_inv():
                inv_root(k_ss[:, 1, :], k_ss[:, 0, :], ALU.max, 1e-24, k_summed, 1, k_inv)

            for b in range(NB + LAGS):
                if b == 0:
                    keys_inv()
                run(p7, b - 5, 2)
                run(p8, b - 5, 1)
                run(p6, b - 5, 2)
                run(p4, b - 2, 0)
                run(p8, b - 5, 2)
                run(p1, b - 2, 1)
                run(p5, b - 2, 0)
                run(r3, b - 6)
                run(p7, b - 4, 0)
                run(p1, b - 1, 0)
                run(p6, b - 4, 1)
                run(p2, b - 2, 1)
                run(p7, b - 4, 1)
                run(p3, b - 2, 1)
                run(p2, b - 1, 0)
                run(p4, b - 2, 1)
                run(p8, b - 4, 0)
                run(p5, b - 2, 1)
                run(p3, b - 1, 0)
                if b == 1:
                    masks()
                run(p6, b - 3, 0)

        @block.scalar
        def _(act):
            act.dma_start(k_sb[:, :, :], k_weight.rearrange("(k p) h -> p k h", p=P)).then_inc(k_in, 16)
            act.preload_act_table_set(LN_EXP)
            act.wait_ge(c_in, 16)
            act.activation(c_tmp[:, 0, :], c_sb[:, :], ACT.Exp, scale=-1.0).then_inc(silu_exp, 1)
            act.dma_start(wer[:, :], weg).then_inc(w_in, 16)
            act.wait_ge(mod_ps, 1)
            act.activation(mod_row[:, 0, 1, :], score[:, 0, H:2 * H], ACT.Identity, bias=1.0).then_inc(mod_rows, 1)
            act.activation(mod_row[:, 0, 0, :], score[:, 0, 0:H], ACT.Copy).then_inc(mod_rows, 1)
            act.wait_ge(mod_ps, 2)
            act.activation(mod_row[:, 1:NB, 1, :], score[:, 1:NB, H:2 * H], ACT.Identity, bias=1.0)
            act.activation(mod_row[:, 1:NB, 0, :], score[:, 1:NB, 0:H], ACT.Copy).then_inc(mod_rows, 1)
            act.activation(mod_row[:, :, 2:4, :], score[:, :, 2 * H:4 * H].rearrange("p b (g h) -> p b g h", h=H),
                           ACT.Copy).then_inc(mod_rows, 1)
            act.activation(gate_t[:, 2], score[:, :, 2 * H:4 * H].rearrange("p b (g h) -> p b g h", h=H),
                           ACT.Abs).then_inc(mod_rows, 1)

            def keys_copy():
                act.wait_ge(k_turned, 1)
                act.activation(k_t[:, :], xps[:, :], ACT.Copy).then_inc(k_ready, 1)

            def e1(b, h):
                u = 2 * b + h
                act.wait_ge(q_turned, u + 1)
                if u > 3:
                    act.wait_ge(score_ready, 2 * (u - 3))
                act.activation(q_t[:, b % 2, h * HT:(h + 1) * HT], turn[:, :], ACT.Copy).then_inc(q_evac, 1)

            def r(b, h, p):
                n = 4 * b + 2 * h + p
                t = root[:, p, :]
                act.wait_ge(score_ready, n + 1)
                if n > 1:
                    act.wait_ge(tan_ready, n - 1)
                act.activation(t.rearrange("p (a t) -> p a t", a=2), score[:, 2 * p:2 * p + 2, :],
                               ACT.Square).then_inc(sq_done, 1)
                act.wait_ge(sq_done, n + 1)
                act.activation(t, t, ACT.Ln, scale=-1.0, bias=1.0).then_inc(ln_done, 1)
                act.wait_ge(ln_done, n + 1)
                act.activation(t, t, ACT.Exp, scale=-0.5).then_inc(root_ready, 1)

            def v(b):
                act.preload_act_table_set(TRIG)
                for h in range(2):
                    t = prob[:, b % 2, h].rearrange("p k t -> p (k t)")
                    act.wait_ge(tan_ready, 4 * b + 2 * h + 2)
                    act.activation(t, t, ACT.Arctan).then_inc(atan_done, 1)
                act.preload_act_table_set(LN_EXP)

            def w(b, h):
                n = 2 * b + h
                m, j0, nj = piece(b, h)
                t = prob[:, b % 2, j0 // HJ, :, j0 % HJ * P:(j0 % HJ + nj) * P]
                act.wait_ge(atan_done, min(n, U - 1) + 1)
                act.activation(t, t, ACT.Ln, scale=1.0 / PI, bias=0.5).then_inc(lnp_done, 1)
                act.wait_ge(lnp_done, n + 1)
                act.activation(t, t, ACT.Exp, scale=TAU).then_inc(prob_ready, 1)

            def xs(b, h):
                n = 2 * b + h
                m, j0, nj = piece(b, h)
                act.wait_ge(x_ready, n + 1)
                if n > 1:
                    act.wait_ge(invx_ready, n - 1)
                for j in range(nj):
                    last = act.activation(xsq[:, m, j, :], banks(h)[0][:, j, :], ACT.Square,
                                          accum_out=ss[:, 1, m, j:j + 1])
                last.then_inc(ssx_ready, 1)

            def e2(b, h):
                n = 2 * b + h
                m, j0, nj = piece(b, h)
                act.wait_ge(y_turned, n + 1)
                if n > 1:
                    act.wait_ge(z_ready, n - 1)
                act.activation(y_t[:, m, 0:nj * P], banks(h)[1][:, 0:nj * P], ACT.Copy).then_inc(y_evac, 1)

            def ex(b):
                act.wait_ge(below_ready, b + 1)
                act.activation(rt[:, 1], rt[:, 0], ACT.Exp).then_inc(exp_ready, 1)

            for b in range(NB + LAGS):
                run(xs, b - 3, 0)
                run(r, b - 2, 1, 0)
                run(r, b - 2, 1, 1)
                run(e2, b - 4, 1)
                run(xs, b - 3, 1)
                run(w, b - 3, 2)
                run(e1, b - 1, 0)
                run(e2, b - 4, 2)
                run(v, b - 2)
                run(r, b - 1, 0, 0)
                run(xs, b - 3, 2)
                if b == 0:
                    keys_copy()
                run(ex, b - 4)
                run(w, b - 2, 0)
                run(e1, b - 1, 1)
                run(r, b - 1, 0, 1)
                run(w, b - 2, 1)
                run(e2, b - 3, 0)

        @block.vector
        def _(dve):
            step = [0]

            def link(ins):
                step[0] += 1
                ins.then_inc(dve_step, 1)
                dve.wait_ge(dve_step, step[0])

            def stats(src, i, n):
                m, nj = n % 2, src.shape[1]
                if n > 1:
                    dve.wait_ge(var_ready[i], n - 1)
                for j in range(nj):
                    last = dve.bn_stats(bn[:, i, m, j, :], src[:, j, :])
                link(last)
                for j in range(nj):
                    last = dve.bn_aggr(st[:, i, m, j, :], bn[:, i, m, j, :])
                last.then_inc(var_ready[i], 1)

            def square_sums(dst, products, src, signal):
                for j in range(HJ):
                    last = dve.tensor_tensor_reduce(products[:, j, :], src[:, j, :], src[:, j, :], 1.0, 0.0,
                                                    ALU.mult, ALU.add, dst[:, j:j + 1])
                last.then_inc(signal, 1)

            def normed(dst, src, i, m, signal):
                for j in range(src.shape[1]):
                    last = dve.tensor_scalar(dst[:, j, :], src[:, j, :], st[:, i, m, j, 0:1], rs[:, i, m, j:j + 1],
                                             ALU.subtract, ALU.mult)
                last.then_inc(signal, 1)

            def a1(b, h):
                dve.wait_ge(x_in[b], 16)
                u = 2 * b + h
                if u > 1:
                    dve.wait_ge(norm1_ready, u - 1)
                stats(xin[:, b, half(h), :], 0, u)

            def modulated(dst, mid, src, i, h, factor, offset, ready, count, signal):
                dve.wait_ge(var_ready[i], count)
                for j in range(HJ):
                    last = dve.scalar_tensor_tensor(out=mid[:, j, :], in0=src[:, j, :], scalar=st[:, i, h, j, 0:1],
                                                    in1=factor, op0=ALU.subtract, op1=ALU.mult)
                link(last)
                dve.wait_ge(ready, count)
                for j in range(HJ):
                    last = dve.scalar_tensor_tensor(out=dst[:, j, :], in0=mid[:, j, :], scalar=rs[:, i, h, j:j + 1],
                                                    in1=offset, op0=ALU.mult, op1=ALU.add)
                last.then_inc(signal, 1)

            def a2(b, h):
                u = 2 * b + h
                if u < FAST:
                    dve.wait_ge(mod_rows, 2)
                    modulated(yh[:, h], ya[:, h], xin[:, b, half(h), :], 0, h, mod_row[:, b, 1, :], mod_row[:, b, 0, :],
                              inv_ready[0], u + 1, norm1_ready)
                    return
                dve.wait_ge(inv_ready[0], u + 1)
                if u > FAST + 1:
                    dve.wait_ge(h_ready, u - 1 - FAST)
                normed(ya[:, h], xin[:, b, half(h), :], 0, h, norm1_ready)

            def a3(b, h):
                u = 2 * b + h
                if u < FAST:
                    dve.wait_ge(norm1_ready, u + 1)
                else:
                    dve.wait_ge(h_ready, u + 1 - FAST)
                stats(yh[:, h], 1, u)

            def a4(b, h):
                u = 2 * b + h
                if u < FAST:
                    dve.wait_ge(rows_in, 16)
                    modulated(yg[:, h], ya[:, h], yh[:, h], 1, h, lnw, lnb, inv_ready[1], u + 1, norm2_ready)
                    return
                dve.wait_ge(inv_ready[1], u + 1)
                if u > 1:
                    dve.wait_ge(q_ready, u - 1)
                normed(yg[:, h], yh[:, h], 1, h, norm2_ready)

            def a5(b, h):
                u = 2 * b + h
                if u < FAST:
                    dve.wait_ge(norm2_ready, u + 1)
                else:
                    dve.wait_ge(g_ready, u + 1 - FAST)
                if u > 1:
                    dve.wait_ge(invq_ready, u - 1)
                square_sums(ss[:, 0, h], gsq[:, h], yg[:, h], ssq_ready)

            def a6(b, h):
                u = 2 * b + h
                dve.wait_ge(invq_ready, u + 1)
                if u > 1:
                    dve.wait_ge(q_turned, u - 1)
                dve.tensor_tensor(yq[:, h], yg[:, h], rs[:, 3, h].unsqueeze(2).to_broadcast([P, HJ, H]),
                                  ALU.mult).then_inc(q_ready, 1)

            def g(b, h, p):
                n = 4 * b + 2 * h + p
                dve.wait_ge(root_ready, n + 1)
                if b > 1:
                    dve.wait_ge(x_ready, 2 * (b - 2) + h + 1)
                dve.scalar_tensor_tensor(out=prob[:, b % 2, h, 2 * p:2 * p + 2, :],
                                         in0=root[:, p, :].rearrange("p (a t) -> p a t", a=2), scalar=TAN_MAX,
                                         in1=score[:, 2 * p:2 * p + 2, :],
                                         op0=ALU.min, op1=ALU.mult).then_inc(tan_ready, 1)

            def xe(b, h):
                n = 2 * b + h
                m, j0, nj = piece(b, h)
                if n == 0:
                    dve.wait_ge(gate_ready, 1)
                dve.wait_ge(ssx_ready, n + 1)
                if n > 1:
                    dve.wait_ge(x1_ready, n - 1)
                dve.tensor_tensor(xa[:, m, 0:nj], banks(h)[0][:, 0:nj], gates[:, b, 0:1, :].to_broadcast([P, nj, H]),
                                  ALU.mult).then_inc(xps_used, 1)

            def c2(b, h):
                n = 2 * b + h
                m, j0, nj = piece(b, h)
                dve.wait_ge(invx_ready, n + 1)
                dve.wait_ge(xres_ready, n + 1)
                dve.wait_ge(xps_used, n + 1)
                if b > 1:
                    dve.wait_ge(res_ready, min(n, U - 1) - 3)
                for j in range(nj):
                    last = dve.scalar_tensor_tensor(out=x1[:, b % 2, j0 + j, :], in0=xa[:, m, j, :],
                                                    scalar=rs[:, 4, m, j:j + 1], in1=xres[:, m, j, :],
                                                    op0=ALU.mult, op1=ALU.add)
                last.then_inc(x1_ready, 1)

            def c3(b, h):
                m, j0, nj = piece(b, h)
                dve.wait_ge(x1_ready, 2 * b + h + 1)
                stats(x1[:, b % 2, j0:j0 + nj, :], 2, 2 * b + h)

            def c4(b, h):
                n = 2 * b + h
                m, j0, nj = piece(b, h)
                dve.wait_ge(inv_ready[2], n + 1)
                if n > 1:
                    dve.wait_ge(y_turned, n - 1)
                normed(yc[:, m], x1[:, b % 2, j0:j0 + nj, :], 2, m, y_ready)

            def ze(b, h):
                n = 2 * b + h
                m, j0, nj = piece(b, h)
                dve.wait_ge(z_ready, n + 1)
                if b > 1:
                    dve.wait_ge(res_ready, 2 * (b - 1))
                zb = banks(h)[2]
                for i in range(nj // 2):
                    t = slice(j0 + 2 * i, j0 + 2 * i + 2)
                    dve.tensor_tensor(logit[:, b % 2, t, :], zb[:, i, :, H:W],
                                      const_b[:, b:b + 1, H:W].to_broadcast([P, 2, E]), ALU.add)
                    last = dve.tensor_tensor(z_sb[:, b % 2, t, :], zb[:, i, :, 0:H],
                                             const_b[:, b:b + 1, 0:H].to_broadcast([P, 2, H]), ALU.add)
                last.then_inc(z_used, 1)

            def wide(col):
                return col.unsqueeze(2).to_broadcast([P, J, E])

            def r1(b):
                lg = logit[:, b % 2]
                dve.wait_ge(z_used, 2 * b + 2 if b < NB - 1 else U + 1)
                link(dve.tensor_reduce(rc[:, 0, :], lg, AX.X, ALU.max))
                dve.tensor_tensor(rt[:, 0], lg, wide(rc[:, 0, :]), ALU.subtract).then_inc(below_ready, 1)
                link(dve.tensor_tensor(rt[:, 2], lg, wide(rc[:, 0, :]), ALU.is_equal))
                link(dve.tensor_tensor(rt[:, 3], rt[:, 2], rank[:, :].unsqueeze(1).to_broadcast([P, J, E]), ALU.mult))
                link(dve.tensor_reduce(rc[:, 1, :], rt[:, 3], AX.X, ALU.max))
                dve.tensor_tensor(hot[:, :, :], rt[:, 3], wide(rc[:, 1, :]), ALU.is_equal).then_inc(hot_ready, 1)
                if b < NB - 1:
                    dve.wait_ge(hot_ready, b + 1)
                    link(dve.tensor_reduce(rt[:, 4, 0, :], hot[:, :, :].rearrange("p j e -> p e j"), AX.X, ALU.add))
                    dve.tensor_tensor(taken[:, (b + 1) % 2, :], taken[:, b % 2, :], rt[:, 4, 0, :],
                                      ALU.add).then_inc(taken_ready, 1)

            def r2(b):
                dve.wait_ge(exp_ready, b + 1)
                link(dve.tensor_reduce(rc[:, 2, :], rt[:, 1], AX.X, ALU.add))
                dve.reciprocal(rc[:, 3, :], rc[:, 2, :])
                dve.wait_ge(place_ready, b + 1)
                link(dve.scalar_tensor_tensor(out=rt[:, 5], in0=place, scalar=CAP, in1=hot[:, :, :],
                                              op0=ALU.is_le, op1=ALU.mult))
                link(dve.tensor_reduce(rc[:, 4, :], rt[:, 5], AX.X, ALU.add))
                dve.tensor_tensor(keep_gate[:, b % 2, :], rc[:, 4, :], rc[:, 3, :], ALU.mult).then_inc(gate_col_ready, 1)

            def r3(b):
                if b < NB - 1:
                    return
                dve.wait_ge(gate_col_ready, b + 1)
                dve.wait_ge(out_done[b - 2], 32)
                for h in range(2):
                    if h == 0:
                        dve.wait_ge(res_ready, 2 * b)
                    for j in range(h * HJ, (h + 1) * HJ):
                        last = dve.scalar_tensor_tensor(out=res[:, b % 2, j, :], in0=z_sb[:, b % 2, j, :],
                                                        scalar=keep_gate[:, b % 2, j:j + 1], in1=x1[:, b % 2, j, :],
                                                        op0=ALU.mult, op1=ALU.add)
                    last.then_inc(res_ready, 1)

            def silu():
                dve.wait_ge(silu_exp, 1)
                link(dve.tensor_scalar(c_tmp[:, 1, :], c_tmp[:, 0, :], 1.0, None, ALU.add))
                link(dve.reciprocal(c_tmp[:, 2, :], c_tmp[:, 1, :]))
                link(dve.tensor_tensor(silu_t[:, :], c_sb[:, :], c_tmp[:, 2, :], ALU.mult))
                for bs in (slice(0, 1), slice(1, NB)):
                    n = bs.stop - bs.start
                    dve.tensor_copy(silu_b[:, bs, :],
                                    silu_t[:, bs].unsqueeze(2).to_broadcast([P, n, P])).then_inc(silu_wide, 1)

            def keys_sum():
                dve.wait_ge(k_in, 16)
                square_sums(k_ss[:, 0, :], k_sq, k_sb, k_summed)

            def keys_scale():
                dve.wait_ge(k_inv, 1)
                dve.tensor_tensor(k_unit[:, :, :], k_sb[:, :, :], k_ss[:, 1, :].unsqueeze(2).to_broadcast([P, KC, H]),
                                  ALU.mult).then_inc(k_scaled, 1)

            def mod_columns():
                dve.wait_ge(mod_cols, 1)
                dve.tensor_copy(modc[:, 0, :], turn[:, 0:NB])
                dve.tensor_scalar(modc[:, 1, :], turn[:, NB:2 * NB], 1.0, None, ALU.add).then_inc(modc_ready, 1)

            def gate_rows():
                dve.wait_ge(mod_rows, 5)
                gr = mod_row[:, :, 2:4, :]
                two, sign, size = (gate_t[:, i] for i in range(3))
                link(dve.tensor_scalar(two, gr, 0.0, 2.0, ALU.is_ge, ALU.mult))
                link(dve.tensor_scalar(sign, two, -1.0, None, ALU.add))
                flat = [t.rearrange("p b g h -> p (b g h)") for t in (gates[:, :, :, :], size, sign)]
                dve.scalar_tensor_tensor(out=flat[0], in0=flat[1], scalar=0.25, in1=flat[2],
                                         op0=ALU.max, op1=ALU.mult).then_inc(gate_ready, 1)
                dve.wait_ge(gate_ready, 1)
                dve.wait_ge(rows_in, 16)
                dve.tensor_tensor(gate_bias[:, :, :], gates[:, :, 0, :],
                                  bias_b.unsqueeze(1).to_broadcast([P, NB, H]), ALU.mult).then_inc(gate_bias_ready, 1)

            def fold_weights():
                dve.wait_ge(modc_ready, 1)
                dve.tensor_copy(shift2_b[:, :, :], modc[:, 0, :].unsqueeze(2).to_broadcast([P, NB, P])).then_inc(shift2_ready, 1)
                dve.wait_ge(w_in, 16)
                for b in range(NB):
                    dve.scalar_tensor_tensor(out=wer_b[:, b, 0:H], in0=wer[:, 0:H], scalar=modc[:, 1, b:b + 1],
                                             in1=gates[:, b, 1, :], op0=ALU.mult, op1=ALU.mult)
                    last = dve.tensor_scalar(wer_b[:, b, H:W], wer[:, H:W], modc[:, 1, b:b + 1], None, ALU.mult)
                last.then_inc(wer_ready, 1)

            def fold_constants():
                dve.wait_ge(const_ps, 1)
                for i in range(2):
                    dve.tensor_tensor(const_b[:, 2 * i:2 * i + 2, 0:H], zview[:, i, :, 0:H],
                                      be_b.unsqueeze(1).to_broadcast([P, 2, H]), ALU.add)
                    last = dve.tensor_copy(const_b[:, 2 * i:2 * i + 2, H:W], zview[:, i, :, H:W])
                link(last)
                dve.tensor_tensor(const_b[:, :, 0:H], const_b[:, :, 0:H], gates[:, :, 1, :], ALU.mult).then_inc(const_ready, 1)

            dve.memset(taken[:, :, :], 0.0).then_inc(taken_ready, 1)
            silu()
            for b in range(NB + LAGS):
                run(a2, b - 1, 0)
                run(ze, b - 5, 2)
                if b == 1:
                    keys_scale()
                run(a4, b - 2, 1)
                if b == 3:
                    gate_rows()
                run(c2, b - 4, 1)
                run(c3, b - 4, 1)
                run(r1, b - 5)
                run(a5, b - 2, 1)
                run(a3, b - 1, 0)
                run(a6, b - 2, 1)
                if b == 3:
                    fold_weights()
                run(c4, b - 4, 0)
                run(r2, b - 5)
                run(a1, b - 1, 1)
                if b == 0:
                    keys_sum()
                run(xe, b - 4, 2)
                run(g, b - 2, 0, 0)
                run(r3, b - 6)
                run(a4, b - 1, 0)
                run(a1, b, 0)
                run(c2, b - 4, 2)
                run(c3, b - 4, 2)
                run(c4, b - 4, 1)
                run(g, b - 2, 0, 1)
                run(a5, b - 1, 0)
                if b == 4:
                    fold_constants()
                run(a2, b - 1, 1)
                run(xe, b - 3, 0)
                run(ze, b - 4, 0)
                run(c2, b - 3, 0)
                run(g, b - 2, 1, 0)
                run(c4, b - 4, 2)
                if b == 1:
                    mod_columns()
                run(a6, b - 1, 0)
                run(c3, b - 3, 0)
                run(g, b - 2, 1, 1)
                run(a3, b - 1, 1)
                run(xe, b - 3, 1)
                run(ze, b - 4, 1)

        @block.tensor
        def _(pe):
            pe.wait_ge(silu_wide, 1)
            pe.wait_ge(wmod_first_in, 16)
            pe.matmul(score[:, 0, 0:2 * H], silu_b[:, 0, :], wmod_sb[:, 0:2 * H],
                      start=True, stop=True).then_inc(mod_ps, 1)
            pe.wait_ge(silu_wide, 2)
            pe.wait_ge(wmod_in, 16)
            for b in (*range(1, NB), 0):
                if b > 0:
                    pe.matmul(score[:, b, 0:3 * H], silu_b[:, b, :], wmod_sb[:, 0:3 * H], start=True, stop=True)
                else:
                    pe.wait_ge(mod_rows, 2)
                    pe.matmul(score[:, b, 2 * H:3 * H], silu_b[:, b, :], wmod_sb[:, 2 * H:3 * H], start=True, stop=True)
                last = pe.matmul(score[:, b, 3 * H:4 * H], silu_b[:, b, :], wmod_sb[:, 5 * H:6 * H], start=True, stop=True)
            last.then_inc(mod_ps, 1)
            for i in range(2):
                last = pe.matmul(turn[:, i * NB:(i + 1) * NB], wmod_sb[:, (3 + i) * H:(4 + i) * H], silu_t[:, :],
                                 start=True, stop=True)
            last.then_inc(mod_cols, 1)
            pe.wait_ge(pool_const, 3)

            def keys_turn():
                pe.wait_ge(k_scaled, 1)
                for k in range(KC):
                    last = pe.transpose(xps[:, k * P:(k + 1) * P], k_unit[:, k, :], ident[:, :])
                last.then_inc(k_turned, 1)

            turns = [0, 0]

            def bank_free():
                if turns[0]:
                    pe.wait_ge(q_evac, turns[0])
                else:
                    pe.wait_ge(modc_ready, 1)
                if turns[1]:
                    pe.wait_ge(y_evac, turns[1])

            def t1(b, h):
                pe.wait_ge(q_ready, 2 * b + h + 1)
                bank_free()
                for j in range(HJ):
                    last = pe.transpose(turn[:, j * P:(j + 1) * P], yq[:, h, j, :], ident[:, :])
                last.then_inc(q_turned, 1)
                turns[0] += 1

            def s(b, h, p):
                n = 4 * b + 2 * h + p
                pe.wait_ge(q_evac, 2 * b + h + 1)
                if n == 0:
                    pe.wait_ge(k_ready, 1)
                    pe.wait_ge(mod_rows, 5)
                if n > 1:
                    pe.wait_ge(tan_ready, n - 1)
                for i in range(2):
                    k = 2 * p + i
                    last = pe.matmul(score[:, 2 * p + i, :], k_t[:, k * P:(k + 1) * P],
                                     q_t[:, b % 2, h * HT:(h + 1) * HT], start=True, stop=True)
                last.then_inc(score_ready, 1)

            def x(b, h):
                n = 2 * b + h
                m, j0, nj = piece(b, h)
                pe.wait_ge(prob_ready, n + 1)
                xb = banks(h)[0]
                if n == 0:
                    pe.wait_ge(qw_in, 16)
                elif h < 2:
                    pe.wait_ge(xps_used, n)
                else:
                    pe.wait_ge(tan_ready, 4 * NB)
                for j in range(nj):
                    t = j0 % HJ + j
                    for k in range(KC):
                        last = pe.matmul(xb[:, j, :], prob[:, b % 2, j0 // HJ, k, t * P:(t + 1) * P],
                                         q_w[:, k, :], start=(k == 0), stop=(k == KC - 1))
                last.then_inc(x_ready, 1)

            def keep_clock(b):
                if b < NB - 1:
                    return
                pe.wait_ge(tan_ready, 4 * NB)
                pe.wait_ge(atan_done, 2 * NB)
                for i in range(4):
                    pe.matmul(score[:, i, :], k_t[:, 0:P], k_t[:, :], start=True, stop=True)

            def t2(b, h):
                m, j0, nj = piece(b, h)
                pe.wait_ge(y_ready, 2 * b + h + 1)
                if h < 2:
                    bank_free()
                for j in range(nj):
                    last = pe.transpose(banks(h)[1][:, j * P:(j + 1) * P], yc[:, m, j, :], ident[:, :])
                last.then_inc(y_turned, 1)
                turns[1] += 1

            projected = [0]
            queued = [0]

            def z(b, h):
                n = 2 * b + h
                m, j0, nj = piece(b, h)
                pe.wait_ge(y_evac, n + 1)
                if n == 0:
                    pe.wait_ge(const_ready, 1)
                    pe.wait_ge(wer_ready, 1)
                elif h < 2:
                    pe.wait_ge(z_used, n)
                if queued[0]:
                    pe.wait_ge(gate_col_ready, queued[0])
                for j in range(nj):
                    last = pe.matmul(banks(h)[2][:, j // 2, j % 2, :], y_t[:, m, j * P:(j + 1) * P],
                                     wer_b[:, b, :], start=True, stop=True)
                last.then_inc(z_ready, 1)
                projected[0] = n + 1

            def q(b):
                pe.wait_ge(hot_ready, b + 1)
                pe.wait_ge(taken_ready, b + 1)
                if b == 0:
                    pe.wait_ge(pool_const, 6 + E)
                pe.wait_ge(z_used, projected[0])
                if b > 0:
                    pe.wait_ge(gate_col_ready, b)
                queued[0] = b + 1
                pe.matmul(place, ones[:, :], taken[:, b % 2, :].unsqueeze(1).to_broadcast([P, J, E]),
                          start=True, stop=False)
                for j in range(J):
                    if j > 0:
                        pe.matmul(place[:, 0:j, :], tri_strict[:, :], hot[:, j:j + 1, :].to_broadcast([P, j, E]),
                                  start=False, stop=False)
                    last = pe.matmul(place[:, j:J, :], tri_incl[:, :], hot[:, j:j + 1, :].to_broadcast([P, J - j, E]),
                                     start=False, stop=(j == J - 1))
                last.then_inc(place_ready, 1)

            def constants():
                pe.wait_ge(shift2_ready, 1)
                pe.wait_ge(w_in, 16)
                for b in range(NB):
                    last = pe.matmul(zview[:, b // 2, b % 2, :], shift2_b[:, b, :], wer[:, :], start=True, stop=True)
                last.then_inc(const_ps, 1)

            for b in range(NB + LAGS):
                run(q, b - 5)
                run(s, b - 2, 0, 1)
                run(t1, b - 2, 1)
                if b == 4:
                    constants()
                run(t2, b - 4, 0)
                run(x, b - 3, 0)
                run(s, b - 2, 1, 0)
                run(z, b - 4, 0)
                run(t2, b - 4, 1)
                if b == 1:
                    keys_turn()
                run(s, b - 2, 1, 1)
                run(x, b - 3, 1)
                run(t1, b - 1, 0)
                run(t2, b - 4, 2)
                run(z, b - 4, 1)
                run(s, b - 1, 0, 0)
                run(z, b - 4, 2)
                run(keep_clock, b - 2)
                run(x, b - 3, 2)


def kernel(**inputs):
    import numpy as _np
    import concourse.bacc as _bacc
    from concourse import mybir as _mybir
    from concourse.bass_utils import run_bass_kernel_spmd as _run

    laid = {
        "x": inputs["L0_attn_hidden_states"],
        "c_t": _np.asarray(inputs["L0_c"]).T,
        "rows": _np.stack([inputs["L0_attn_ln_weight"], inputs["L0_attn_ln_bias"], inputs["L0_attn_bias"],
                           inputs["L0_ffn_be"]]),
        "k_weight": inputs["L0_attn_k_weight"],
        "q_weight": inputs["L0_attn_q_weight"],
        "weg": _np.concatenate([inputs["L0_ffn_We"], inputs["L0_ffn_Wg"]], axis=1),
        "wmod": inputs["L0_wmod"],
    }
    nc = _bacc.Bacc("TRN2", target_bir_lowering=False, num_devices=1)
    arrays, args = {}, []
    for name, a in laid.items():
        a = _np.ascontiguousarray(a)
        arrays[f"in_{name}_dram"] = a
        args.append(nc.dram_tensor(f"in_{name}_dram", a.shape, _mybir.dt.from_np(a.dtype), kind="ExternalInput").ap())
    out = nc.dram_tensor("out_0_dram", laid["x"].shape, _mybir.dt.from_np(_np.dtype("float32")), kind="ExternalOutput").ap()
    adaln_block(nc, *args, out)
    r = _run(nc, [arrays], core_ids=[0])
    return r.results[0]["out_0_dram"]
```
